# Optimizing a Trainium2 kernel written in Bass

```python
import numpy as np
import jax
import jax.numpy as jnp

def _softmax(x, axis=-1):
    return jax.nn.softmax(x, axis=axis)

def _gelu(x):
    return jax.nn.gelu(x, approximate=True)

def _silu(x):
    return jax.nn.silu(x)

def _sigmoid(x):
    return jax.nn.sigmoid(x)

def _layernorm(x, axis=-1, eps=1e-05):
    m = jnp.mean(x, axis=axis, keepdims=True)
    v = jnp.var(x, axis=axis, keepdims=True)
    return (x - m) / jnp.sqrt(v + eps)

def _scatter_add(tgt, idx, src, axis=0):
    return tgt.at[idx].add(src)

def _segment_sum(src, seg, n):
    return jax.ops.segment_sum(src, seg, n)
kernel_name = 'mk_prb_d1_jaxref_r8_275fd1'

def setup_inputs(seed: int=0):
    np.random.seed(seed)
    _w = jnp.asarray

    def _L0_attn_setup():
        import jax, jax.numpy as jnp
        import numpy as np
        import math
        N_HEAD = 16
        HEAD_DIM = 64
        N_EMBD = 128
        EPS_RMS = 1e-05
        U_L2_EPS = 1e-06

        def _get_alibi_slopes(n_heads):

            def pow2(n):
                start = 2 ** (-2 ** (-(math.log2(n) - 3)))
                return [start * start ** i for i in range(n)]
            if math.log2(n_heads).is_integer():
                return pow2(n_heads)
            c = 2 ** math.floor(math.log2(n_heads))
            s = pow2(c)
            extra = _get_alibi_slopes(2 * c)
            return s + extra[0::2][:n_heads - c]

        def _rmsnorm(x, w):
            var = jnp.mean(jnp.square(x), axis=-1, keepdims=True)
            return x * jax.lax.rsqrt(var + EPS_RMS) * w
        key = jax.random.key(seed)
        ks = jax.random.split(key, 9)
        B, T = (2, 256)
        H, D, C = (N_HEAD, HEAD_DIM, N_EMBD)
        x = jax.random.normal(ks[0], (B, T, C), dtype=jnp.float32)
        sc = 1.0 / math.sqrt(C)
        Wq = jax.random.normal(ks[1], (C, H * D), dtype=jnp.float32) * sc
        Wk = jax.random.normal(ks[2], (C, H * D), dtype=jnp.float32) * sc
        Wv = jax.random.normal(ks[3], (C, H * D), dtype=jnp.float32) * sc
        Wproj = jax.random.normal(ks[4], (H * D, C), dtype=jnp.float32) * (0.5 / math.sqrt(C) / math.sqrt(12))
        q_rms_w = jnp.ones((D,), dtype=jnp.float32)
        k_rms_w = jnp.ones((D,), dtype=jnp.float32)
        omega = jnp.full((H,), math.log(math.expm1(1.0)), dtype=jnp.float32)
        u = jax.random.normal(ks[5], (H, D), dtype=jnp.float32) * (1.0 / math.sqrt(D))
        return {'x': x, 'Wq': Wq, 'Wk': Wk, 'Wv': Wv, 'Wproj': Wproj, 'q_rms_w': q_rms_w, 'k_rms_w': k_rms_w, 'omega': omega, 'u': u}
    _L0_attn_in = _L0_attn_setup()

    def _L0_ffn_setup():
        import jax, jax.numpy as jnp
        import numpy as np
        TOP_K = 8
        NUM_EXPERTS = 32
        CAPACITY = 128
        key = jax.random.key(seed)
        k1, k2, k3, k4 = jax.random.split(key, 4)
        B, S, H, E, F = (2, 128, 128, NUM_EXPERTS, 96)
        return {'hidden_states': jax.random.normal(k1, (B, S, H), dtype=jnp.float32), 'gate_weight': jax.random.normal(k2, (E, H), dtype=jnp.float32) * 0.02, 'gate_up_proj': jax.random.normal(k3, (E, 2 * F, H), dtype=jnp.float32) * 0.02, 'down_proj': jax.random.normal(k4, (E, H, F), dtype=jnp.float32) * 0.02}
    _L0_ffn_in = _L0_ffn_setup()
    _d = {'L0_attn_x': _L0_attn_in['x'], 'L0_attn_Wq': _L0_attn_in['Wq'], 'L0_attn_Wk': _L0_attn_in['Wk'], 'L0_attn_Wv': _L0_attn_in['Wv'], 'L0_attn_Wproj': _L0_attn_in['Wproj'], 'L0_attn_q_rms_w': _L0_attn_in['q_rms_w'], 'L0_attn_k_rms_w': _L0_attn_in['k_rms_w'], 'L0_attn_omega': _L0_attn_in['omega'], 'L0_attn_u': _L0_attn_in['u'], 'L0_ffn_gate_weight': _L0_ffn_in['gate_weight'], 'L0_ffn_gate_up_proj': _L0_ffn_in['gate_up_proj'], 'L0_ffn_down_proj': _L0_ffn_in['down_proj']}
    _x0 = _d['L0_attn_x']
    _d['L0_attn_x'] = jax.random.normal(jax.random.fold_in(jax.random.key(seed), 1), (2, 1024, 128), dtype=_x0.dtype)
    del _x0
    return _d

def reference(L0_attn_x, L0_attn_Wq, L0_attn_Wk, L0_attn_Wv, L0_attn_Wproj, L0_attn_q_rms_w, L0_attn_k_rms_w, L0_attn_omega, L0_attn_u, L0_ffn_gate_weight, L0_ffn_gate_up_proj, L0_ffn_down_proj):

    def _L0_attn_ref(x, Wq, Wk, Wv, Wproj, q_rms_w, k_rms_w, omega, u):
        import jax, jax.numpy as jnp
        import numpy as np
        import math
        N_HEAD = 16
        HEAD_DIM = 64
        N_EMBD = 128
        EPS_RMS = 1e-05
        U_L2_EPS = 1e-06

        def _get_alibi_slopes(n_heads):

            def pow2(n):
                start = 2 ** (-2 ** (-(math.log2(n) - 3)))
                return [start * start ** i for i in range(n)]
            if math.log2(n_heads).is_integer():
                return pow2(n_heads)
            c = 2 ** math.floor(math.log2(n_heads))
            s = pow2(c)
            extra = _get_alibi_slopes(2 * c)
            return s + extra[0::2][:n_heads - c]

        def _rmsnorm(x, w):
            var = jnp.mean(jnp.square(x), axis=-1, keepdims=True)
            return x * jax.lax.rsqrt(var + EPS_RMS) * w
        B, T, C = x.shape
        H, D = (N_HEAD, HEAD_DIM)
        q = (x @ Wq).reshape(B, T, H, D)
        k = (x @ Wk).reshape(B, T, H, D)
        v = (x @ Wv).reshape(B, T, H, D)
        q = _rmsnorm(q, q_rms_w)
        k = _rmsnorm(k, k_rms_w)
        slopes = jnp.asarray(_get_alibi_slopes(H), dtype=jnp.float32)
        omega_eff = jax.nn.softplus(omega) * slopes
        u_n = u / jnp.maximum(jnp.linalg.norm(u, axis=-1, keepdims=True), U_L2_EPS)
        gate_logits = jnp.einsum('bthd,hd->bht', k, u_n) / math.sqrt(D)
        gate = jax.nn.softplus(gate_logits)
        idx = jnp.arange(T)
        dist = jnp.maximum(idx[:, None] - idx[None, :], 0).astype(jnp.float32)
        bias = -dist[None, None] * omega_eff[None, :, None, None] * gate[:, :, None, :]
        causal = idx[:, None] >= idx[None, :]
        bias = jnp.where(causal[None, None], bias, -jnp.inf)
        scale = 1.0 / math.sqrt(D)
        scores = jnp.einsum('bihd,bjhd->bhij', q, k) * scale + bias
        attn = jax.nn.softmax(scores, axis=-1)
        y = jnp.einsum('bhij,bjhd->bihd', attn, v).reshape(B, T, H * D)
        return y @ Wproj

    def _L0_ffn_ref(hidden_states, gate_weight, gate_up_proj, down_proj):
        import jax, jax.numpy as jnp
        import numpy as np
        TOP_K = 8
        NUM_EXPERTS = 32
        CAPACITY = 128
        B, S, H = hidden_states.shape
        E = gate_weight.shape[0]
        N = B * S
        x = hidden_states.reshape(N, H)
        logits = x @ gate_weight.T
        probs = jax.nn.softmax(logits.astype(jnp.float32), axis=-1)
        topw, topi = jax.lax.top_k(probs, TOP_K)
        topw = topw / topw.sum(-1, keepdims=True)
        topw = topw.astype(x.dtype)
        flat_e = topi.reshape(-1)
        flat_w = topw.reshape(-1)
        flat_x = jnp.repeat(x, TOP_K, axis=0)
        oh = jax.nn.one_hot(flat_e, E, dtype=jnp.int32)
        pos = (jnp.cumsum(oh, axis=0) * oh).sum(-1) - 1
        buf = jnp.zeros((E, CAPACITY, H), x.dtype).at[flat_e, pos].set(flat_x, mode='drop')
        gu = jnp.einsum('ech,efh->ecf', buf, gate_up_proj)
        gate, up = jnp.split(gu, 2, axis=-1)
        h = jax.nn.silu(gate) * up
        eo = jnp.einsum('ecf,ehf->ech', h, down_proj)
        tok_out = eo.at[flat_e, pos].get(mode='fill', fill_value=0)
        out = (tok_out * flat_w[:, None]).reshape(N, TOP_K, H).sum(1)
        return out.reshape(B, S, H)
    x = L0_attn_x
    xn = _layernorm(x, axis=-1)
    x = x + _L0_attn_ref(xn, L0_attn_Wq, L0_attn_Wk, L0_attn_Wv, L0_attn_Wproj, L0_attn_q_rms_w, L0_attn_k_rms_w, L0_attn_omega, L0_attn_u) + _L0_ffn_ref(xn, L0_ffn_gate_weight, L0_ffn_gate_up_proj, L0_ffn_down_proj)
    return x

_drawn_inputs = setup_inputs


def setup_inputs(seed=0):
    import zlib

    import numpy as np

    out = dict(_drawn_inputs(seed))
    spreads = {'L0_attn_q_rms_w': (1.0, 0.6),
     'L0_attn_k_rms_w': (1.0, 0.6),
     'L0_attn_omega': (0.5413248538970947, 0.6)}
    factors = {'L0_attn_u': 6.942,
     'L0_ffn_gate_weight': 8.0,
     'L0_ffn_gate_up_proj': 8.0,
     'L0_ffn_down_proj': 8.0}
    for name, (base, spread) in spreads.items():
        noise = np.random.default_rng([zlib.crc32(name.encode()), seed]).standard_normal(out[name].shape)
        drawn = base * np.exp(spread * noise) if base else spread * noise
        out[name] = jnp.asarray(drawn.astype(out[name].dtype))
    for name, factor in factors.items():
        out[name] = (out[name] * factor).astype(out[name].dtype)
    return out
```

```python
import concourse.bass as bass
from concourse import mybir
from contextlib import ExitStack

B, T, C = 2, 1024, 128
H, D = 16, 64
E, TOPK, CAP, F = 32, 8, 128, 96
P = 128
N = B * T
NT = N // P
TB = T // P
NPAIR = B * H // 2
ROW = C + E
NROWS = N + CAP
CH = 512
AUG = 64
MROW = 96
NEG = -1.0e30

K_ID, K_MR, K_MT, K_NP, K_SLOT, K_ONES, K_UM, K_SL, K_OWN = 0, 128, 256, 384, 385, 513, 641, 643, 675
K_END = K_OWN + CAP // 4

MAXC = []
for _ib in range(TB):
    _w = P * (_ib + 1)
    if _w > CH:
        MAXC += [(_ib, 0, CH, False), (_ib, CH, _w - CH, True)]
    else:
        MAXC += [(_ib, 0, _w, True)]
STC = []
for _jb in range(TB):
    for _c in range(2):
        _q0 = max(P * _jb, CH * _c)
        if _q0 < CH * (_c + 1):
            STC += [(_jb, _c, _q0, CH * (_c + 1) - _q0, _q0 == P * _jb)]
NC = len(STC)
assert NC == len(MAXC) == 12

PREP = ["q0", "q1", "k0", "k1", "v0", "v1", "nq0", "nq1", "nk0", "nk1", "vt0", "vt1", "gate", "aug0", "aug1"]
MOE = ["mx", "mgu", "meo"]
USES = {
    "PRO": PREP + ["mb"],
    "FIRST": PREP[:12] + ["ma"] + PREP[12:] + MOE + ["mb"],
    "MID": PREP[:6] + ["pr0", "pr1"] + PREP[6:12] + ["ma"] + PREP[12:] + MOE + ["mb"],
    "LAST": ["pr0", "pr1", "ma"] + MOE,
    "FIN": ["pr0", "pr1"] + [f"ft{i}" for i in range(4)],
}
N_PRO, N_FIRST, N_MID, N_LAST = (len(USES[k]) for k in ("PRO", "FIRST", "MID", "LAST"))
assert N_PRO % 2 == 0 and N_FIRST % 2 == 0 and N_MID % 2 == 0 and N_LAST % 2 == 0


def use(kind, s, name):
    k = USES[kind].index(name)
    if kind == "PRO":
        base, half = 0, 0
    elif kind == "FIRST":
        base, half = N_PRO, N_PRO // 2
    elif kind == "MID":
        base = (s - 1) * N_MID + (N_PRO + N_FIRST)
        half = (s - 1) * (N_MID // 2) + (N_PRO + N_FIRST) // 2
    else:
        base = N_PRO + N_FIRST + (NPAIR - 2) * N_MID
        if kind == "FIN":
            base += N_LAST
        half = base // 2
    return k % 2, base + k + 1, half + k // 2


def wait(eng, sem, value):
    if isinstance(value, int) and value <= 0:
        return
    eng.wait_ge(sem, value)


def layer(nc, x, w3, wproj, qw, kw, om, u, gwt, gup, dwn, cst, augq, out):
    f32, r32, bf16, u32 = mybir.dt.float32, mybir.dt.float32r, mybir.dt.bfloat16, mybir.dt.uint32
    ALU, ACT, AX = mybir.AluOpType, mybir.ActivationFunctionType, mybir.AxisListType
    ctx = ExitStack()
    with ctx:
        def sb(name, shape, dt=f32):
            return ctx.enter_context(nc.sbuf_tensor(name, shape, dt))

        def sem(name):
            return ctx.enter_context(nc.semaphore(name))

        table = nc.dram_tensor("token_table", [NROWS, ROW], f32).ap()
        total = nc.dram_tensor("residual_and_experts", [NROWS, C], f32).ap()

        K = sb("consts", [P, K_END])
        ident = K[:, K_ID:K_ID + P]
        neg_p = K[:, K_NP:K_NP + 1]
        slot_no = K[:, K_SLOT:K_SLOT + P]
        blk_ones = K[:, K_ONES:K_ONES + P]
        head_of = K[:, K_UM:K_UM + 2]
        slopes = K[:, K_SL:K_SL + 2 * NPAIR]
        own_slot_no = K[:, K_OWN:K_OWN + CAP // 4]
        maskb = sb("mask_bf16", [P, 3 * P], bf16)
        ident_b, mask_qk, mask_kq = maskb[:, 0:P], maskb[:, P:2 * P], maskb[:, 2 * P:3 * P]
        qwk = sb("qk_norm_weights", [P, 3])
        omE = sb("minus_omega", [P, 3, 2 * NPAIR])
        uc = sb("u_columns", [P, 3, NPAIR])
        U2 = sb("u_pair", [P, 2, 2])
        eps = sb("eps", [P, 2])
        gw = sb("router_weight", [P, E])

        X = sb("x", [P, NT, C])
        XW = sb("token_rows", [P, NT, ROW])
        xh, xl = sb("xn_hi", [P, N], r32), sb("xn_lo", [P, N], r32)
        stats = sb("stats", [P, NT, 6])
        mv = sb("mean_var", [P, NT, 2])
        rs = sb("ln_rstd", [P, 2, NT])

        wraw = sb("w_raw", [P, 3 * P])
        wh, wl = sb("w_hi", [P, 3 * P], r32), sb("w_lo", [P, 3 * P], r32)
        RAW = sb("qk", [P, 2, T])
        SQ = sb("qk_sq", [P, 2, T])
        HL = sb("qk_parts", [P, 4, T], r32)
        HI, LO = HL[:, 0:2, :], HL[:, 2:4, :]
        vT = sb("vT", [P, T])
        GT = sb("gate_work", [P, 6, 2 * TB])
        R = sb("bias_columns", [P, TB, P])
        QM, KM, QX, KX = ([sb(f"{n}{i}", [P, 2, T], r32) for i in range(2)] for n in ("QM", "KM", "QX", "KX"))
        V = [sb(f"V{i}", [P, TB, 2, P]) for i in range(2)]

        mx = sb("row_max_halves", [P, 4, 2])
        mcol = sb("row_max", [P, TB])
        mrow = sb("minus_max_row", [TB, 2, P], r32)
        PR = sb("probs", [P, 4, CH])
        RL = sb("inverse_sums", [D, 2, T])
        Y = sb("y", [P, T])
        AQ = Y
        wp = sb("w_proj", [P, C])
        acc = sb("attn_out_T", [P, N])

        idxT = sb("slot_token", [P, E], u32)
        idxc = [sb(f"slot_token_pair{i}", [P, 2], u32) for i in range(2)]
        G = [sb(f"gathered{i}", [P, 2, ROW]) for i in range(2)]
        wgu = [sb(f"w_gate_up{i}", [P, 2, 2 * F]) for i in range(2)]
        wdn = [sb(f"w_down{i}", [F, 2, C]) for i in range(2)]
        XG = sb("gathered_T", [P, 2 * CAP])
        SG = sb("silu_work", [F, 3, 2 * CAP])
        YW = sb("expert_rows", [P, 2, C])
        ZR = sb("zero_rows", [P, ROW])

        xf = LO[:, :, :].rearrange("p a t -> p (a t)").bitcast(f32)
        CUM = HL[:, :, :].rearrange("p a t -> p (a t)").bitcast(f32)[:, 0:N + CAP]
        prob = SQ[:, 0, 0:NT * E].rearrange("p (t e) -> p t e", e=E)
        repl = SQ[:, 0, NT * E:2 * NT * E].rearrange("p (t e) -> p t e", e=E)
        chosen = SQ[:, 1, 0:NT * E].rearrange("p (t e) -> p t e", e=E)
        selr = RAW[:, 0, :].bitcast(bf16)[:, 0:NT * P].rearrange("p (t g e) -> p t g e", g=4, e=E)
        tops = sb("top8", [P, NT, TOPK])
        rsum = sb("router_sums", [P, 3, NT])
        idx = sb("slot_token_T", [P, E], u32)
        ONES = RAW[:, 1, 0:CH]

        SM = ctx.enter_context(nc.psum_tensor("SM", [P, 2, CH], f32))
        ST = ctx.enter_context(nc.psum_tensor("ST", [P, 2, CH], f32))
        AV = ctx.enter_context(nc.psum_tensor("AV", [P, T], f32))
        XB = ctx.enter_context(nc.psum_tensor("XB", [P, 2, CH], f32))

        S = {n: sem(n) for n in (
            "const_in", "x_in", "w_in", "wp_in", "we_in", "gather_in", "table_out", "total_out", "out_out",
            "consts_ready", "mask_ready", "stats_ready", "ln_var", "ln_rstd", "xn_ready", "zero_ready",
            "xt_psum", "xt_copied", "xh_ready", "xl_ready", "logit_psum", "logit_done", "selr_ready",
            "selT_psum", "selT_done", "idx_ready", "rt", "rt_exp", "omega_exp", "omega_ready", "u_sq",
            "u_psum", "u_ln", "u_ready", "rows_ready", "v_ones", "wts_ready", "pool_c", "pool_steps", "sp_steps",
            "spare_ready", "spare_free0", "spare_free1",
            "w_hi_ready", "w_lo_ready", "raw_ready", "sq_ready", "rs_ln", "rs_ready", "qk_ready", "hi_ready",
            "lo_ready", "spread_done", "vt_ready", "v_ready", "u2_ready", "gl_ready", "gate_abs", "gate_exp",
            "gate_ln", "gs", "bias_ready", "bias_rows_ready",
            "max_scores", "max_taken", "max_half", "max_ready", "mrow_ready", "mrow_in", "scores", "probs_ready",
            "pv_done", "sum_ln", "sum_inv", "y_ready", "proj_added",
            "idxc_ready", "xg_ready", "sg_exp", "sg", "h_ready", "yw_ready", "scatter_done", "final_ready", "res_in")}
        spare_free = [S["spare_free0"], S["spare_free1"]]
        block = ctx.enter_context(nc.Block())

        N_CONST = 8 + 4 * 3 + 0
        SPREAD = 12

        def batch(s):
            return s // (H // 2)

        def pair(s):
            return s % (H // 2)

        @block.sync
        def _(sp):
            sp.dma_start(X[:, :, :], x.rearrange("(t p) c -> p t c", p=P)).then_inc(S["x_in"], 16)
            for dst, src in ((K[:, :], cst), (AQ[:, :], augq), (qwk[:, 0:1], qw), (qwk[:, 1:2], kw),
                             (omE[:, 0, :], om), (uc[:, 0, :], u), (gw[:, :], gwt)):
                sp.dma_start(dst, src).then_inc(S["const_in"], 16)

            def stand(value):
                if not isinstance(value, int):
                    sp.sem_inc(S["sp_steps"], 1)

            def load_w(s, wait_for):
                if wait_for is not None:
                    wait(sp, S["w_hi_ready"], wait_for)
                    wait(sp, S["w_lo_ready"], wait_for)
                sp.dma_start(wraw[:, :], w3[bass.ds(pair(s), 1), :, :].rearrange("a p n -> (a p) n")
                             ).then_inc(S["w_in"], 16)

            def spread(s, b):
                wait(sp, S["pv_done"], NC * (2 * s - 2))
                stand(s)
                for t in (0, 1):
                    sp.wait_ge(S["hi_ready"], 2 * s + t + 1)
                    main, cross = ((QM, QX), (KM, KX))[t]
                    for a in range(2):
                        src = HI[D * a:D * a + D, t, :].bitcast(f32)
                        sp.dma_start(main[b][0:D, a, :].bitcast(f32), src).then_inc(S["spread_done"], 16)
                        sp.dma_start(cross[b][D * (1 - t):D * (2 - t), a, :].bitcast(f32), src).then_inc(S["spread_done"], 16)
                    sp.wait_ge(S["lo_ready"], 2 * s + t + 1)
                    for a in range(2):
                        sp.dma_start(cross[b][D * t:D * t + D, a, :].bitcast(f32), LO[D * a:D * a + D, t, :].bitcast(f32)
                                     ).then_inc(S["spread_done"], 16)

            def load_experts(s, b):
                if not isinstance(s, int) or s >= 2:
                    sp.wait_ge(S["yw_ready"], s - 1)
                sp.dma_start(wgu[b][:, :, :], gup[bass.ds(s, 1), :, :].rearrange("a p (e n) -> (a p) e n", e=2)
                             ).then_inc(S["we_in"], 16)
                sp.dma_start(wdn[b][:, :, :], dwn[bass.ds(s, 1), :, :].rearrange("a p (e n) -> (a p) e n", e=2)
                             ).then_inc(S["we_in"], 16)

            load_w(0, None)
            sp.wait_ge(S["zero_ready"], 1)
            sp.dma_start(table[N:NROWS, :], ZR[:, :]).then_inc(S["table_out"], 16)
            sp.dma_start(total[N:NROWS, :], ZR[:, 0:C]).then_inc(S["total_out"], 16)
            sp.wait_ge(S["x_in"], 16)
            sp.dma_start(total[0:N, :].rearrange("(t p) c -> p t c", p=P), X[:, :, :]).then_inc(S["total_out"], 16)
            sp.wait_ge(S["wts_ready"], 1)
            sp.dma_start(table[0:N, :].rearrange("(t p) c -> p t c", p=P), XW[:, :, :]).then_inc(S["table_out"], 16)
            spread(0, 0)

            def period(s, b, kind):
                if kind != "LAST":
                    load_w(s + 1, s + 1)
                load_experts(s, b)
                if kind != "LAST":
                    spread(s + 1, 1 - b)
                if kind != "FIRST":
                    _, ready, _ = use(kind, s, "pr1")
                    sp.wait_ge(S["spare_ready"], ready)
                sp.dma_start(wp[:, :], wproj[bass.ds(pair(s), 1), :, :].rearrange("a p n -> (a p) n")
                             ).then_inc(S["wp_in"], 16)

            period(0, 0, "FIRST")
            with sp.Fori(0, (NPAIR - 2) // 2) as it:
                period(2 * it + 1, 1, "MID")
                period(2 * it + 2, 0, "MID")
            period(NPAIR - 1, 1, "LAST")
            sp.wait_ge(S["scatter_done"], 32 * NPAIR)
            sp.dma_start(X[:, :, :], total[0:N, :].rearrange("(t p) c -> p t c", p=P)).then_inc(S["res_in"], 16)
            for g in range(4):
                sp.wait_ge(S["final_ready"], g + 1)
                sp.dma_start(out[g * CH:(g + 1) * CH, :].rearrange("(t p) c -> p t c", p=P),
                             XW[:, 4 * g:4 * g + 4, 0:C]).then_inc(S["out_out"], 16)
            sp.wait_ge(S["out_out"], 64)
            sp.wait_ge(S["table_out"], 32)
            sp.wait_ge(S["total_out"], 32)

        @block.tensor
        def _(pe):
            mm = nc.tensor.matmul

            def mm3(o, whi, wlo, xhi, xlo):
                mm(o, wlo, xhi, start=True, stop=False)
                mm(o, whi, xlo, start=False, stop=False)
                return mm(o, whi, xhi, start=False, stop=True)

            def spare(kind, s, name):
                bank, ready, earlier = use(kind, s, name)
                wait(pe, spare_free[bank], earlier)
                return XB[:, bank, :]

            def project(kind, s, name, buf_s):
                o = spare(kind, s, name)
                i, c = "qkv".index(name[0]), int(name[1])
                col = batch(buf_s) * T + c * CH
                w = slice(i * P, (i + 1) * P)
                mm3(o, wh[:, w], wl[:, w], xh[:, bass.ds(col, CH)], xl[:, bass.ds(col, CH)]
                    ).then_inc(S["spare_ready"], 1)

            def head_norm(kind, s, name):
                o = spare(kind, s, name)
                t, c = "qk".index(name[1]), int(name[2])
                mm(o, blk_ones, SQ[:, t, c * CH:(c + 1) * CH], start=True, stop=True).then_inc(S["spare_ready"], 1)

            def v_back(kind, s, name):
                o = spare(kind, s, name)
                c = int(name[2])
                for j in range(4):
                    last = nc.tensor.transpose(o[:, j * P:(j + 1) * P], vT[:, c * CH + j * P:c * CH + (j + 1) * P], ident)
                last.then_inc(S["spare_ready"], 1)

            def gate(kind, s):
                o = spare(kind, s, "gate")
                for j in range(TB):
                    last = mm(o[:, 2 * j:2 * j + 2], RAW[:, 1, j * P:(j + 1) * P], U2[:, 0, :], start=True, stop=True)
                last.then_inc(S["spare_ready"], 1)

            def bias_rows(kind, s, name):
                o = spare(kind, s, name)
                c = int(name[3])
                for j in range(4):
                    last = nc.tensor.transpose(o[:, j * P:(j + 1) * P], R[:, 4 * c + j, :], ident)
                last.then_inc(S["spare_ready"], 1)

            def prep(kind, s, p, step):
                if step == 1:
                    pe.wait_ge(S["w_hi_ready"], p + 1)
                    pe.wait_ge(S["w_lo_ready"], p + 1)
                    for n in ("q0", "q1"):
                        project(kind, s, n, p)
                elif step == 2:
                    for n in ("k0", "k1"):
                        project(kind, s, n, p)
                elif step == 3:
                    for n in ("v0", "v1"):
                        project(kind, s, n, p)
                elif step == 5:
                    pe.wait_ge(S["sq_ready"], 2 * p + 1)
                    for n in ("nq0", "nq1"):
                        head_norm(kind, s, n)
                elif step == 6:
                    pe.wait_ge(S["sq_ready"], 2 * p + 2)
                    for n in ("nk0", "nk1"):
                        head_norm(kind, s, n)
                elif step == 7:
                    pe.wait_ge(S["vt_ready"], 2 * p + 2)
                    for n in ("vt0", "vt1"):
                        v_back(kind, s, n)
                elif step == 9:
                    pe.wait_ge(S["qk_ready"], 2 * p + 2)
                    pe.wait_ge(S["u2_ready"], p + 1)
                    gate(kind, s)
                elif step == 11:
                    pe.wait_ge(S["bias_ready"], p + 1)
                    for n in ("aug0", "aug1"):
                        bias_rows(kind, s, n)

            def max_chunk(n, b, a, i):
                ib, j0, w, diag = MAXC[i]
                wait(pe, S["max_taken"], NC * n + i - 1)
                o = SM[:, i % 2, 0:w]
                last = mm(o, QM[b][0:MROW, a, ib * P:(ib + 1) * P], KM[b][0:MROW, a, j0:j0 + w],
                          start=True, stop=not diag)
                if diag:
                    last = mm(SM[:, i % 2, w - P:w], ident_b, mask_qk, start=False, stop=True)
                last.then_inc(S["max_scores"], 1)

            def max_row(kind, s, name, n):
                o = spare(kind, s, name)
                pe.wait_ge(S["max_ready"], n + 1)
                nc.tensor.transpose(o[0:TB, 0:P], mcol[:, :], ident).then_inc(S["spare_ready"], 1)

            def score_chunk(n, b, a, i):
                jb, c, q0, w, diag = STC[i]
                wait(pe, S["probs_ready"], NC * n + i - 1)
                o = ST[:, i % 2, 0:w]
                keys = slice(jb * P, (jb + 1) * P)
                mm(o, KX[b][:, a, keys], QX[b][:, a, q0:q0 + w], start=True, stop=False)
                last = mm(o, KM[b][0:MROW + 1, a, keys], QM[b][0:MROW + 1, a, q0:q0 + w], start=False, stop=not diag)
                if diag:
                    last = mm(ST[:, i % 2, 0:P], ident_b, mask_kq, start=False, stop=True)
                last.then_inc(S["scores"], 1)

            def moe_step(kind, s, b, step):
                if step == 1:
                    pe.wait_ge(S["gather_in"], 32 * (s + 1))
                    o = spare(kind, s, "mx")
                    for e in range(2):
                        last = nc.tensor.transpose(o[:, e * P:(e + 1) * P], G[b][:, e, 0:C], ident)
                    last.then_inc(S["spare_ready"], 1)
                elif step == 3:
                    pe.wait_ge(S["xg_ready"], s + 1)
                    pe.wait_ge(S["we_in"], 32 * (s + 1))
                    o = spare(kind, s, "mgu")
                    for gu in range(2):
                        for e in range(2):
                            at = gu * 2 * CAP + e * CAP
                            last = mm(o[0:F, at:at + CAP], wgu[b][:, e, gu * F:(gu + 1) * F],
                                      XG[:, e * CAP:(e + 1) * CAP], start=True, stop=True)
                    last.then_inc(S["spare_ready"], 1)
                elif step == 7:
                    pe.wait_ge(S["h_ready"], s + 1)
                    o = spare(kind, s, "meo")
                    for e in range(2):
                        last = mm(o[:, e * C:(e + 1) * C], SG[:, 2, e * CAP:(e + 1) * CAP], wdn[b][:, e, :],
                                  start=True, stop=True)
                    last.then_inc(S["spare_ready"], 1)

            def project_out(kind, s, p):
                pe.wait_ge(S["y_ready"], 2 * p + 2)
                pe.wait_ge(S["wp_in"], 16 * (p + 1))
                for c in range(2):
                    o = spare(kind, s, f"pr{c}")
                    mm(o, wp[:, :], Y[:, c * CH:(c + 1) * CH], start=True, stop=True).then_inc(S["spare_ready"], 1)

            pe.wait_ge(S["consts_ready"], 1)
            pe.wait_ge(S["u_sq"], 1)
            mm(AV[:, 0:NPAIR], blk_ones, uc[:, 1, :], start=True, stop=True).then_inc(S["u_psum"], 1)
            for g in range(4):
                pe.wait_ge(S["xn_ready"], g + 1)
                wait(pe, S["xt_copied"], g - 1)
                for j in range(4):
                    last = nc.tensor.transpose(ST[:, g % 2, j * P:(j + 1) * P], XW[:, 4 * g + j, 0:C], ident)
                last.then_inc(S["xt_psum"], 1)
            for t in range(NT):
                if t % 4 == 0:
                    pe.wait_ge(S["xt_copied"], t // 4 + 1)
                last = mm(SM[:, 0, t * E:(t + 1) * E], xf[:, t * P:(t + 1) * P], gw[:, :], start=True, stop=True)
            last.then_inc(S["logit_psum"], 1)
            pe.wait_ge(S["selr_ready"], 1)
            pe.wait_ge(S["mask_ready"], 1)
            for g in range(4):
                if g >= 2:
                    pe.wait_ge(S["selT_done"], g - 1)
                for j in range(4):
                    last = mm(ST[:, g % 2, j * P:(j + 1) * P],
                              selr[:, 4 * g + j, :, :].rearrange("p g e -> p (g e)"), ident_b, start=True, stop=True)
                last.then_inc(S["selT_psum"], 1)
            pe.wait_ge(S["selT_done"], 4)
            pe.wait_ge(S["xh_ready"], 4)
            pe.wait_ge(S["xl_ready"], 4)
            pe.wait_ge(S["u_ready"], 1)
            for step in range(NC):
                prep("PRO", 0, 0, step)

            def first_use(p, with_rows):
                pe.wait_ge(S["spread_done"], 16 * SPREAD * (p + 1))
                pe.wait_ge(S["bias_rows_ready"], 4 * (p + 1))
                if with_rows:
                    pe.wait_ge(S["rows_ready"], 8)

            first_use(0, True)
            for i in range(NC):
                max_chunk(0, 0, 0, i)
            max_row("PRO", 0, "mb", 0)

            def slot(s, b, a, kind, nxt):
                n = 2 * s + a
                nb = b if a == 0 else 1 - b
                pe.wait_ge(S["mrow_in"], 16 * (n + 1))
                for i in range(NC + 2):
                    if i < NC:
                        score_chunk(n, b, a, i)
                    if nxt and i < 6:
                        if i == 0 and a == 1:
                            first_use(s + 1, False)
                        for k in (2 * i, 2 * i + 1):
                            max_chunk(n + 1, nb, 1 - a, k)
                    if i < NC and a == 0 and kind != "LAST":
                        prep(kind, s, s + 1, i)
                    if a == 0 and i == 4 and kind != "FIRST":
                        project_out(kind, s, s - 1)
                    if a == 1:
                        moe_step(kind, s, b, i)
                    if i == 8 and nxt:
                        max_row(kind, s, "ma" if a == 0 else "mb", n + 1)
                    if i >= 2:
                        if i == 2:
                            pe.wait_ge(S["v_ready"], 2 * s + 2)
                            wait(pe, S["y_ready"], n)
                        jb, c, q0, w, _ = STC[i - 2]
                        pe.wait_ge(S["probs_ready"], NC * n + i - 1)
                        mm(AV[:, q0:q0 + w], V[b][:, jb, a, :], PR[:, (i - 2) % 4, 0:w],
                           start=(jb == 0), stop=(jb == 4 * c + 3)).then_inc(S["pv_done"], 1)

            def period(s, b, kind):
                slot(s, b, 0, kind, True)
                slot(s, b, 1, kind, kind != "LAST")

            pe.wait_ge(S["v_ones"], 1)
            period(0, 0, "FIRST")
            with pe.Fori(0, (NPAIR - 2) // 2) as it:
                period(2 * it + 1, 1, "MID")
                period(2 * it + 2, 0, "MID")
            period(NPAIR - 1, 1, "LAST")
            project_out("FIN", 0, NPAIR - 1)
            pe.wait_ge(S["proj_added"], 2 * NPAIR)
            for g in range(4):
                o = spare("FIN", 0, f"ft{g}")
                for j in range(4):
                    t = 4 * g + j
                    last = nc.tensor.transpose(o[:, j * P:(j + 1) * P], acc[:, t * P:(t + 1) * P], ident)
                last.then_inc(S["spare_ready"], 1)

        @block.scalar
        def _(act):
            fn = nc.scalar.activation

            def taken(kind, s, name):
                bank, ready, _ = use(kind, s, name)
                act.wait_ge(S["spare_ready"], ready)
                return XB[:, bank, :], spare_free[bank]

            def prep(kind, s, p, pb, step):
                if step == 0:
                    act.wait_ge(S["w_in"], 16 * (p + 1))
                    if kind != "PRO":
                        act.wait_ge(S["vt_ready"], 2 * p)
                    fn(wh[:, :], wraw[:, :], ACT.Copy).then_inc(S["w_hi_ready"], 1)
                elif step in (2, 3):
                    t = step - 2
                    act.wait_ge(S["raw_ready"], 2 * (2 * p + t + 1))
                    wait(act, S["qk_ready"], 2 * p + t - 1)
                    fn(SQ[:, t, :], RAW[:, t, :], ACT.Square).then_inc(S["sq_ready"], 1)
                elif step == 4:
                    for c in range(2):
                        o, free = taken(kind, s, f"v{c}")
                        fn(vT[:, c * CH:(c + 1) * CH], o, ACT.Copy).then_inc(S["vt_ready"], 1)
                        act.wait_ge(S["vt_ready"], 2 * p + c + 1)
                        act.sem_inc(free, 1)
                elif step in (6, 7):
                    t = step - 6
                    for c in range(2):
                        o, free = taken(kind, s, f"n{'qk'[t]}{c}")
                        fn(SQ[:, t, c * CH:(c + 1) * CH], o, ACT.Ln, bias=eps[:, 0:1]).then_inc(free, 1)
                        act.wait_ge(free, use(kind, s, f"n{'qk'[t]}{c}")[2] + 1)
                    fn(SQ[:, t, :], SQ[:, t, :], ACT.Exp, scale=-0.5).then_inc(S["rs_ready"], 1)
                elif step == 8:
                    wait(act, S["pv_done"], NC * (2 * p - 2))
                    for c in range(2):
                        o, free = taken(kind, s, f"vt{c}")
                        fn(V[pb][:, 4 * c:4 * c + 4, :, 0:D], o.rearrange("p (j a d) -> p j a d", j=4, a=2),
                           ACT.Copy).then_inc(S["v_ready"], 1)
                        act.wait_ge(S["v_ready"], 2 * p + c + 1)
                        act.sem_inc(free, 1)
                elif step == 9:
                    act.wait_ge(S["gl_ready"], p + 1)
                    fn(GT[:, 1, :], GT[:, 0, :], ACT.Abs).then_inc(S["gate_abs"], 1)
                    act.wait_ge(S["gate_abs"], p + 1)
                    fn(GT[:, 2, :], GT[:, 1, :], ACT.Exp, scale=-1.0).then_inc(S["gate_exp"], 1)
                    act.wait_ge(S["gate_exp"], p + 1)
                    fn(GT[:, 1, :], GT[:, 2, :], ACT.Ln, bias=1.0).then_inc(S["gate_ln"], 1)
                elif step == 11:
                    wait(act, S["pv_done"], NC * (2 * p - 2))
                    for c in range(2):
                        o, free = taken(kind, s, f"aug{c}")
                        for a in range(2):
                            fn(KM[pb][AUG:AUG + 32, a, c * CH:(c + 1) * CH], o[AUG + 32 * a:AUG + 32 * a + 32, :],
                               ACT.Copy).then_inc(S["bias_rows_ready"], 1)
                        act.wait_ge(S["bias_rows_ready"], 4 * p + 2 * c + 2)
                        act.sem_inc(free, 1)

            def max_row(kind, s, name, n, b, a, par):
                o, free = taken(kind, s, name)
                wait(act, S["mrow_in"], 16 * (n - 1))
                fn(mrow[:, par, :], o[0:TB, 0:P], ACT.Copy, scale=-1.0).then_inc(S["mrow_ready"], 1)
                act.wait_ge(S["mrow_ready"], n + 1)
                act.sem_inc(free, 1)
                act.dma_start(QM[b][MROW:MROW + 1, a, :].rearrange("o (k q) -> o k q", q=P).bitcast(f32),
                              mrow[:, par, :].bitcast(f32)).then_inc(S["mrow_in"], 16)

            def inverse_sums(n):
                act.wait_ge(S["pv_done"], NC * (n + 1))
                wait(act, S["y_ready"], n)
                fn(RL[:, 0, :], AV[D:2 * D, :], ACT.Ln).then_inc(S["sum_ln"], 1)
                act.wait_ge(S["sum_ln"], n + 1)
                fn(RL[:, 1, :], RL[:, 0, :], ACT.Exp, scale=-1.0).then_inc(S["sum_inv"], 1)

            def moe_step(kind, s, step):
                if step == 2:
                    o, free = taken(kind, s, "mx")
                    fn(XG[:, :], o[:, 0:2 * CAP], ACT.Copy).then_inc(S["xg_ready"], 1)
                    act.wait_ge(S["xg_ready"], s + 1)
                    act.sem_inc(free, 1)
                elif step == 4:
                    bank, ready, _ = use(kind, s, "mgu")
                    act.wait_ge(S["spare_ready"], ready)
                    fn(SG[:, 0, :], XB[0:F, bank, 0:2 * CAP], ACT.Exp, scale=-1.0).then_inc(S["sg_exp"], 1)

            act.wait_ge(S["const_in"], 16 * 7)
            act.wait_ge(S["pool_c"], 2)
            fn(omE[:, 1, :], omE[:, 0, :], ACT.Abs).then_inc(S["omega_exp"], 1)
            act.wait_ge(S["omega_exp"], 1)
            fn(omE[:, 2, :], omE[:, 1, :], ACT.Exp, scale=-1.0).then_inc(S["omega_exp"], 1)
            act.wait_ge(S["omega_exp"], 2)
            fn(omE[:, 1, :], omE[:, 2, :], ACT.Ln, bias=1.0).then_inc(S["omega_exp"], 1)
            act.wait_ge(S["ln_var"], NT)
            fn(rs[:, 0, :], mv[:, :, 1], ACT.Ln, bias=eps[:, 0:1]).then_inc(S["ln_rstd"], 1)
            act.wait_ge(S["ln_rstd"], 1)
            fn(rs[:, 1, :], rs[:, 0, :], ACT.Exp, scale=-0.5).then_inc(S["ln_rstd"], 1)
            act.wait_ge(S["u_ln"], 1)
            fn(uc[:, 2, :], uc[:, 1, :], ACT.Ln).then_inc(S["u_ln"], 1)
            act.wait_ge(S["u_ln"], 2)
            fn(uc[:, 1, :], uc[:, 2, :], ACT.Exp, scale=-0.5).then_inc(S["u_ln"], 1)
            for g in range(4):
                act.wait_ge(S["xt_copied"], g + 1)
                fn(xh[:, g * CH:(g + 1) * CH], xf[:, g * CH:(g + 1) * CH], ACT.Copy).then_inc(S["xh_ready"], 1)
            act.wait_ge(S["rt_exp"], 1)
            fn(prob, chosen, ACT.Exp).then_inc(S["rt_exp"], 1)
            act.wait_ge(S["idx_ready"], 1)
            act.wait_ge(S["xl_ready"], 4)
            for step in range(NC):
                prep("PRO", 0, 0, 0, step)
            max_row("PRO", 0, "mb", 0, 0, 0, 0)

            def slot(s, b, a, kind, nxt):
                n = 2 * s + a
                if not (kind == "FIRST" and a == 0):
                    inverse_sums(n - 1)
                for i in range(NC):
                    jb, c, q0, w, _ = STC[i]
                    act.wait_ge(S["scores"], NC * n + i + 1)
                    wait(act, S["pv_done"], NC * n + i - 3)
                    fn(PR[:, i % 4, 0:w], ST[:, i % 2, 0:w], ACT.Exp).then_inc(S["probs_ready"], 1)
                    if a == 0 and kind != "LAST":
                        prep(kind, s, s + 1, 1 - b, i)
                    if a == 1:
                        moe_step(kind, s, i)
                    if i == 8 and nxt:
                        nb = b if a == 0 else 1 - b
                        max_row(kind, s, "ma" if a == 0 else "mb", n + 1, nb, 1 - a, 1 - a)

            def period(s, b, kind):
                slot(s, b, 0, kind, True)
                slot(s, b, 1, kind, kind != "LAST")

            period(0, 0, "FIRST")
            with act.Fori(0, (NPAIR - 2) // 2) as it:
                period(2 * it + 1, 1, "MID")
                period(2 * it + 2, 0, "MID")
            period(NPAIR - 1, 1, "LAST")
            inverse_sums(2 * NPAIR - 1)

        @block.vector
        def _(dve):
            v = nc.vector

            def taken(kind, s, name):
                bank, ready, _ = use(kind, s, name)
                dve.wait_ge(S["spare_ready"], ready)
                return XB[:, bank, :], spare_free[bank]

            def diag(row0):
                full = R[:, :, :]
                return bass.AP(full.tensor, AUG + row0, [[TB * P, P], [P + 1, TB], [32, 2]])

            def gate_bias(p):
                def step(k):
                    return GS * p + k
                GS = 4
                dve.wait_ge(S["gate_ln"], p + 1)
                v.scalar_tensor_tensor(GT[:, 3, :], GT[:, 0, :], 0.0, GT[:, 1, :], op0=ALU.max, op1=ALU.add
                                       ).then_inc(S["gs"], 1)
                dve.wait_ge(S["gs"], step(1))
                v.tensor_tensor(GT[:, 4, :].rearrange("p (j a) -> p j a", a=2),
                                GT[:, 3, :].rearrange("p (j a) -> p j a", a=2),
                                omE[:, 0, bass.ds(2 * p, 2)].unsqueeze(1).to_broadcast([P, TB, 2]), ALU.mult
                                ).then_inc(S["gs"], 1)
                dve.wait_ge(S["gs"], step(2))
                g3 = GT[:, 4, :].rearrange("p (j a) -> p j a", a=2)
                j3 = GT[:, 5, :].rearrange("p (j a) -> p j a", a=2)
                v.tensor_scalar(GT[:, 5, :], GT[:, 4, :], neg_p, None, ALU.mult).then_inc(S["gs"], 1)
                v.tensor_copy(diag(0).bitcast(r32), g3)
                dve.wait_ge(S["gs"], step(3))
                Rv = R[:, :, AUG:AUG + 64].rearrange("p j (a r) -> p j a r", a=2)
                v.tensor_copy(Rv[:, :, :, 16].bitcast(r32), j3).then_inc(S["gs"], 1)
                dve.wait_ge(S["gs"], step(4))
                v.tensor_tensor(diag(8), g3, diag(0), ALU.subtract)
                v.tensor_tensor(Rv[:, :, :, 17], j3, Rv[:, :, :, 16], ALU.subtract).then_inc(S["bias_ready"], 1)

            def prep(kind, s, p, step):
                if step == 0:
                    dve.wait_ge(S["w_hi_ready"], p + 1)
                    v.tensor_tensor(wl[:, :], wraw[:, :], wh[:, :].bitcast(f32), ALU.subtract
                                    ).then_inc(S["w_lo_ready"], 1)
                    v.tensor_scalar(U2[:, 0, :], head_of, uc[:, 0, bass.ds(p, 1)], None, ALU.mult
                                    ).then_inc(S["u2_ready"], 1)
                elif step in (1, 2):
                    t = step - 1
                    wait(dve, S["lo_ready"], 2 * p - 1 + t)
                    for c in range(2):
                        o, free = taken(kind, s, f"{'qk'[t]}{c}")
                        v.tensor_copy(RAW[:, t, c * CH:(c + 1) * CH], o).then_inc(S["raw_ready"], 1)
                        dve.wait_ge(S["raw_ready"], 4 * p + 2 * t + c + 1)
                        dve.sem_inc(free, 1)
                elif step in (7, 8):
                    t = step - 7
                    dve.wait_ge(S["rs_ready"], 2 * p + t + 1)
                    v.scalar_tensor_tensor(RAW[:, t, :], RAW[:, t, :], qwk[:, 2 - t:3 - t], SQ[:, t, :],
                                           op0=ALU.mult, op1=ALU.mult).then_inc(S["qk_ready"], 1)
                elif step == 9:
                    o, free = taken(kind, s, "gate")
                    v.tensor_copy(GT[:, 0, :], o[:, 0:2 * TB]).then_inc(S["gl_ready"], 1)
                    dve.wait_ge(S["gl_ready"], p + 1)
                    dve.sem_inc(free, 1)
                elif step == 10:
                    gate_bias(p)

            def max_chunk(n, i):
                ib, j0, w, _ = MAXC[i]
                dve.wait_ge(S["max_scores"], NC * n + i + 1)
                o = mcol[:, ib:ib + 1] if ib < 4 else mx[:, ib - 4, j0 // CH:j0 // CH + 1]
                if i == 0:
                    wait(dve, S["mrow_ready"], n)
                last = v.tensor_reduce(o, SM[:, i % 2, 0:w], axis=AX.X, op=ALU.max).then_inc(S["max_taken"], 1)
                if i == NC - 1:
                    dve.wait_ge(S["max_taken"], NC * (n + 1))
                    v.tensor_tensor(mcol[:, 4:8], mx[:, :, 0], mx[:, :, 1], ALU.max).then_inc(S["max_ready"], 1)

            def normalise(n, a, p):
                dve.wait_ge(S["sum_inv"], n + 1)
                if a == 0 and (not isinstance(p, int) or p >= 1):
                    dve.wait_ge(S["proj_added"], 2 * p)
                v.tensor_tensor(Y[D * a:D * a + D, :], AV[0:D, :], RL[:, 1, :], ALU.mult).then_inc(S["y_ready"], 1)

            def add_projection(kind, s, p):
                for c in range(2):
                    o, free = taken(kind, s, f"pr{c}")
                    dst = acc[:, bass.ds(batch(p) * T + c * CH, CH)]
                    v.tensor_tensor(dst, o, dst, ALU.add).then_inc(S["proj_added"], 1)
                    dve.wait_ge(S["proj_added"], 2 * p + c + 1)
                    dve.sem_inc(free, 1)

            def moe_step(kind, s, b, step):
                if step == 5:
                    bank, ready, _ = use(kind, s, "mgu")
                    up = XB[0:F, bank, 2 * CAP:4 * CAP]
                    gt = XB[0:F, bank, 0:2 * CAP]
                    dve.wait_ge(S["sg_exp"], s + 1)
                    v.tensor_scalar(SG[:, 1, :], SG[:, 0, :], 1.0, None, ALU.add).then_inc(S["sg"], 1)
                    dve.wait_ge(S["sg"], 3 * s + 1)
                    v.reciprocal(SG[:, 0, :], SG[:, 1, :]).then_inc(S["sg"], 1)
                    dve.wait_ge(S["sg"], 3 * s + 2)
                    v.tensor_tensor(SG[:, 1, :], gt, SG[:, 0, :], ALU.mult).then_inc(S["sg"], 1)
                    dve.wait_ge(S["sg"], 3 * s + 3)
                    v.tensor_tensor(SG[:, 2, :], up, SG[:, 1, :], ALU.mult).then_inc(S["h_ready"], 1)
                    dve.wait_ge(S["h_ready"], s + 1)
                    dve.sem_inc(spare_free[bank], 1)
                elif step == 8:
                    o, free = taken(kind, s, "meo")
                    wait(dve, S["scatter_done"], 32 * s)
                    for e in range(2):
                        last = v.tensor_scalar(YW[:, e, :], o[:, e * C:(e + 1) * C],
                                               G[b][:, e, bass.ds(2 * s + (C + e), 1)], None, ALU.mult)
                    last.then_inc(S["yw_ready"], 1)
                    dve.wait_ge(S["yw_ready"], s + 1)
                    dve.sem_inc(free, 1)

            count = [0]

            def rt(ins):
                count[0] += 1
                ins.then_inc(S["rt"], 1)
                dve.wait_ge(S["rt"], count[0])

            dve.wait_ge(S["x_in"], 16)
            for t in range(NT):
                v.bn_stats(stats[:, t, :], X[:, t, :]).then_inc(S["stats_ready"], 1)
            dve.wait_ge(S["stats_ready"], NT)
            for t in range(NT):
                v.bn_aggr(mv[:, t, :], stats[:, t, :]).then_inc(S["ln_var"], 1)
            dve.wait_ge(S["const_in"], 16 * 7)
            v.tensor_copy(maskb[:, :], K[:, 0:3 * P]).then_inc(S["mask_ready"], 1)
            rt(v.tensor_tensor(uc[:, 1, :], uc[:, 0, :], uc[:, 0, :], ALU.mult))
            dve.sem_inc(S["u_sq"], 1)
            dve.sem_inc(S["consts_ready"], 1)
            rt(v.tensor_scalar(qwk[:, 2:3], qwk[:, 0:1], 0.125, None, ALU.mult))
            dve.wait_ge(S["ln_rstd"], 2)
            dve.wait_ge(S["ln_var"], NT)
            for t in range(NT):
                last = v.tensor_scalar(XW[:, t, 0:C], X[:, t, :], mv[:, t, 0:1], rs[:, 1, t:t + 1],
                                       ALU.subtract, ALU.mult)
                if t % 4 == 3:
                    last.then_inc(S["xn_ready"], 1)
            dve.wait_ge(S["u_psum"], 1)
            v.tensor_scalar(uc[:, 1, :], AV[:, 0:NPAIR], float(D), 1e-12, ALU.mult, ALU.max).then_inc(S["u_ln"], 1)
            for g in range(4):
                dve.wait_ge(S["xt_psum"], g + 1)
                v.tensor_copy(xf[:, g * CH:(g + 1) * CH], ST[:, g % 2, :]).then_inc(S["xt_copied"], 1)
            dve.wait_ge(S["u_ln"], 3)
            rt(v.tensor_scalar(uc[:, 1, :], uc[:, 1, :], 0.125, None, ALU.mult))
            v.tensor_tensor(uc[:, 0, :], uc[:, 0, :], uc[:, 1, :], ALU.mult).then_inc(S["u_ready"], 1)
            dve.wait_ge(S["u_ready"], 1)
            dve.wait_ge(S["omega_exp"], 3)
            rt(v.scalar_tensor_tensor(omE[:, 2, :], omE[:, 0, :], 0.0, omE[:, 1, :], op0=ALU.max, op1=ALU.add))
            rt(v.tensor_tensor(omE[:, 0, :], omE[:, 2, :], slopes, ALU.mult))
            for g in range(4):
                dve.wait_ge(S["xh_ready"], g + 1)
                v.tensor_tensor(xl[:, g * CH:(g + 1) * CH], xf[:, g * CH:(g + 1) * CH],
                                xh[:, g * CH:(g + 1) * CH].bitcast(f32), ALU.subtract).then_inc(S["xl_ready"], 1)
            for b in range(2):
                for a in range(2):
                    v.tensor_copy(QM[b][AUG:MROW, a, :], AQ[AUG:MROW, :]).then_inc(S["rows_ready"], 1)
                    v.tensor_copy(KM[b][MROW:MROW + 1, a, :], AQ[MROW:MROW + 1, :]).then_inc(S["rows_ready"], 1)
            dve.wait_ge(S["logit_psum"], 1)
            lg = SM[:, 0, :].rearrange("p (t e) -> p t e", e=E)
            rt(v.tensor_reduce(rsum[:, 0, :], lg, axis=AX.X, op=ALU.max))
            v.tensor_tensor(chosen, lg, rsum[:, 0, :].unsqueeze(2).to_broadcast([P, NT, E]), ALU.subtract
                            ).then_inc(S["rt_exp"], 1)
            dve.wait_ge(S["rt_exp"], 2)
            for t in range(NT):
                v.max(tops[:, t, :], prob[:, t, :]).then_inc(S["logit_done"], 1)
            dve.wait_ge(S["logit_done"], NT)
            for t in range(NT):
                v.match_replace(repl[:, t, :], tops[:, t, :], prob[:, t, :], -1.0).then_inc(S["logit_done"], 1)
            dve.wait_ge(S["logit_done"], 2 * NT)
            rt(v.tensor_scalar(chosen, repl, 0.0, None, ALU.is_lt))
            for g in range(4):
                last = v.tensor_copy(selr[:, :, g, :], chosen)
            last.then_inc(S["selr_ready"], 1)
            rt(v.tensor_tensor(repl, prob, chosen, ALU.mult))
            rt(v.tensor_reduce(rsum[:, 1, :], repl, axis=AX.X, op=ALU.add))
            rt(v.reciprocal(rsum[:, 2, :], rsum[:, 1, :]))
            v.tensor_tensor(XW[:, :, C:ROW], repl, rsum[:, 2, :].unsqueeze(2).to_broadcast([P, NT, E]), ALU.mult
                            ).then_inc(S["wts_ready"], 1)
            v.tensor_copy(CUM[:, N:N + CAP], slot_no)
            rt(v.memset(ONES, 1.0))
            for g in range(4):
                dve.wait_ge(S["selT_psum"], g + 1)
                v.tensor_tensor_scan(CUM[:, g * CH:(g + 1) * CH], ONES, ST[:, g % 2, :],
                                     0.0 if g == 0 else CUM[:, g * CH - 1:g * CH],
                                     ALU.mult, ALU.add).then_inc(S["selT_done"], 1)
                dve.wait_ge(S["selT_done"], g + 1)
            for h in range(4):
                last = v.max_index(idx[:, 8 * h:8 * h + 8], own_slot_no[:, 8 * h:8 * h + 8], CUM)
            rt(last)
            v.transpose(idxT[:, :], idx[:, :]).then_inc(S["idx_ready"], 1)
            dve.wait_ge(S["idx_ready"], 1)
            rt(v.memset(R[:, :, :], 0.0))
            rt(v.memset(acc[:, :], 0.0))

            for step in range(NC):
                prep("PRO", 0, 0, step)
            for i in range(NC):
                max_chunk(0, i)

            def slot(s, b, a, kind, nxt):
                n = 2 * s + a
                if not (kind == "FIRST" and a == 0):
                    normalise(n - 1, 1 - a, s - 1 if a == 0 else s)
                for i in range(NC):
                    if nxt and i < 6:
                        max_chunk(n + 1, 2 * i)
                        max_chunk(n + 1, 2 * i + 1)
                    if a == 0 and kind != "LAST":
                        prep(kind, s, s + 1, i)
                    if a == 0 and i == 5 and kind != "FIRST":
                        add_projection(kind, s, s - 1)
                    if a == 1:
                        moe_step(kind, s, b, i)

            def period(s, b, kind):
                slot(s, b, 0, kind, True)
                slot(s, b, 1, kind, kind != "LAST")

            period(0, 0, "FIRST")
            with dve.Fori(0, (NPAIR - 2) // 2) as it:
                period(2 * it + 1, 1, "MID")
                period(2 * it + 2, 0, "MID")
            period(NPAIR - 1, 1, "LAST")
            normalise(2 * NPAIR - 1, 1, NPAIR - 1)
            add_projection("FIN", 0, NPAIR - 1)
            dve.wait_ge(S["res_in"], 16)
            for g in range(4):
                o, free = taken("FIN", 0, f"ft{g}")
                v.tensor_tensor(XW[:, 4 * g:4 * g + 4, 0:C], o.rearrange("p (t c) -> p t c", c=C),
                                X[:, 4 * g:4 * g + 4, :], ALU.add).then_inc(S["final_ready"], 1)
                dve.wait_ge(S["final_ready"], g + 1)
                dve.sem_inc(free, 1)

        @block.gpsimd
        def _(pool):
            g_ = nc.gpsimd

            def stand(value):
                if not isinstance(value, int):
                    pool.sem_inc(S["pool_steps"], 1)
            g_.memset(ZR[:, :], 0.0).then_inc(S["zero_ready"], 1)
            g_.memset(eps[:, :], 1e-5).then_inc(S["pool_c"], 2)
            g_.memset(V[0][:, :, :, D:2 * D], 1.0)
            g_.memset(V[1][:, :, :, D:2 * D], 1.0).then_inc(S["v_ones"], 1)

            def split(p):
                for t in range(2):
                    pool.wait_ge(S["qk_ready"], 2 * p + t + 1)
                    stand(p)
                    wait(pool, S["spread_done"], 16 * SPREAD * p)
                    stand(p)
                    g_.tensor_copy(HI[:, t, :], RAW[:, t, :]).then_inc(S["hi_ready"], 1)
                    pool.wait_ge(S["hi_ready"], 2 * p + t + 1)
                    g_.tensor_tensor(LO[:, t, :], RAW[:, t, :], HI[:, t, :].bitcast(f32), ALU.subtract
                                     ).then_inc(S["lo_ready"], 1)

            def gather(s, b):
                if not isinstance(s, int) or s >= 2:
                    pool.wait_ge(S["yw_ready"], s - 1)
                    stand(s)
                g_.tensor_copy(idxc[b][:, :], idxT[:, bass.ds(2 * s, 2)]).then_inc(S["idxc_ready"], 1)
                pool.wait_ge(S["idxc_ready"], s + 1)
                stand(s)
                for e in range(2):
                    g_.indirect_dma_start(out=G[b][:, e, :], out_offset=None, in_=table,
                                          in_offset=bass.IndirectOffsetOnAxis(ap=idxc[b][:, e:e + 1], axis=0)
                                          ).then_inc(S["gather_in"], 16)
                pool.wait_ge(S["gather_in"], 32 * (s + 1))
                stand(s)

            def scatter(s, b):
                pool.wait_ge(S["yw_ready"], s + 1)
                stand(s)
                for e in range(2):
                    g_.indirect_dma_start(out=total,
                                          out_offset=bass.IndirectOffsetOnAxis(ap=idxc[b][:, e:e + 1], axis=0),
                                          in_=YW[:, e, :], in_offset=None, compute_op=ALU.add
                                          ).then_inc(S["scatter_done"], 16)
                    pool.wait_ge(S["scatter_done"], 32 * s + 16 * (e + 1))
                    stand(s)

            pool.wait_ge(S["idx_ready"], 1)
            pool.wait_ge(S["table_out"], 32)
            pool.wait_ge(S["total_out"], 32)
            gather(0, 0)
            split(0)

            def period(s, b, kind):
                if kind != "LAST":
                    split(s + 1)
                scatter(s, b)
                if kind != "LAST":
                    gather(s + 1, 1 - b)

            period(0, 0, "FIRST")
            with pool.Fori(0, (NPAIR - 2) // 2) as it:
                period(2 * it + 1, 1, "MID")
                period(2 * it + 2, 0, "MID")
            period(NPAIR - 1, 1, "LAST")


_INPUTS = ("x", "w3", "wproj", "qw", "kw", "om", "u", "gwt", "gup", "dwn", "cst", "augq")


def _constants(np):
    p, q = np.arange(P)[:, None], np.arange(P)[None, :]
    k = np.zeros((P, K_END), np.float32)
    k[:, K_ID:K_ID + P] = p == q
    k[:, K_MR:K_MR + P] = np.where(q > p, NEG, 0.0)
    k[:, K_MT:K_MT + P] = np.where(p > q, NEG, 0.0)
    k[:, K_NP] = -np.arange(P)
    k[:, K_SLOT:K_SLOT + P] = q + 1
    k[:, K_ONES:K_ONES + P] = (p // D == q // D) / D
    k[:, K_UM:K_UM + 2] = p // D == np.arange(2)[None, :]
    k[:, K_SL:K_SL + 2 * NPAIR] = -np.tile(2.0 ** (-8.0 * (np.arange(H) + 1) / H), B)[None, :]
    k[:, K_OWN:K_OWN + CAP // 4] = 32 * (p // 32) + np.arange(1, CAP // 4 + 1)[None, :]
    a = np.zeros((P, T), np.float32)
    i = np.arange(T)
    for t in range(TB):
        a[AUG + t] = a[AUG + TB + t] = i - P * t
    a[AUG + 2 * TB:AUG + 2 * TB + 2] = 1.0
    a[MROW] = 1.0
    return k, a


def kernel(L0_attn_x, L0_attn_Wq, L0_attn_Wk, L0_attn_Wv, L0_attn_Wproj, L0_attn_q_rms_w, L0_attn_k_rms_w,
           L0_attn_omega, L0_attn_u, L0_ffn_gate_weight, L0_ffn_gate_up_proj, L0_ffn_down_proj):
    import numpy as np
    import concourse.bacc as bacc
    from concourse.bass_utils import run_bass_kernel_spmd

    def pairs(w):
        return np.asarray(w).reshape(C, H // 2, 2 * D).transpose(1, 0, 2)

    cst, augq = _constants(np)
    arrays = {
        "x": np.asarray(L0_attn_x).reshape(N, C),
        "w3": np.concatenate([pairs(L0_attn_Wq), pairs(L0_attn_Wk), pairs(L0_attn_Wv)], axis=2),
        "wproj": np.asarray(L0_attn_Wproj).reshape(H // 2, 2 * D, C),
        "qw": np.tile(np.asarray(L0_attn_q_rms_w), 2)[:, None],
        "kw": np.tile(np.asarray(L0_attn_k_rms_w), 2)[:, None],
        "om": np.broadcast_to(np.tile(np.asarray(L0_attn_omega), B)[None, :], (P, 2 * NPAIR)),
        "u": np.tile(np.asarray(L0_attn_u).reshape(H // 2, 2 * D).T, (1, B)),
        "gwt": np.asarray(L0_ffn_gate_weight).T,
        "gup": np.asarray(L0_ffn_gate_up_proj).reshape(NPAIR, 2, 2 * F, C).transpose(0, 3, 1, 2).reshape(
            NPAIR, C, 4 * F),
        "dwn": np.asarray(L0_ffn_down_proj).reshape(NPAIR, 2, C, F).transpose(0, 3, 1, 2).reshape(NPAIR, F, 2 * C),
        "cst": cst,
        "augq": augq,
    }
    arrays = {k: np.ascontiguousarray(a) for k, a in arrays.items()}
    nc = bacc.Bacc("TRN2", target_bir_lowering=False, num_devices=1)
    ins = [nc.dram_tensor(f"in_{k}", arrays[k].shape, mybir.dt.from_np(arrays[k].dtype), kind="ExternalInput").ap()
           for k in _INPUTS]
    out = nc.dram_tensor("out", (N, C), mybir.dt.float32, kind="ExternalOutput").ap()
    layer(nc, *ins, out)
    r = run_bass_kernel_spmd(nc, [{f"in_{k}": a for k, a in arrays.items()}], core_ids=[0])
    return r.results[0]["out"].reshape(B, T, C)
```

```python
import concourse.bass as bass
from concourse import mybir
from contextlib import ExitStack

B, T, C = 2, 1024, 128
H, D = 16, 64
E, TOPK, CAP, F = 32, 8, 128, 96
P = 128
N = B * T
NT = N // P
TB = T // P
NPAIR = B * H // 2
ROW = C + E
NROWS = N + CAP
CH = 512
AUG = 64
MROW = 96
NEG = -1.0e30

K_ID, K_NP, K_SLOT, K_ONES, K_UM, K_SL, K_OWN = 0, 128, 129, 257, 385, 387, 419
K_END = K_OWN + CAP // 4
K_MR, K_MT, K_ALL = K_END, K_END + P, K_END + 2 * P

MAXC = []
for _ib in range(TB):
    _w = P * (_ib + 1)
    if _w > CH:
        MAXC += [(_ib, 0, CH, False), (_ib, CH, _w - CH, True)]
    else:
        MAXC += [(_ib, 0, _w, True)]
STC = []
for _c in range(2):
    for _jb in range(TB):
        _q0 = max(P * _jb, CH * _c)
        if _q0 < CH * (_c + 1):
            STC += [(_jb, _c, _q0, CH * (_c + 1) - _q0, _q0 == P * _jb)]
NC = len(STC)
HALF_DONE = max(i for i, _s in enumerate(STC) if _s[1] == 0)
LAG = 3
FIRST_MAX = (0, 3)
SUMS = (9, 3)
MAX_ROW = (9, 9)
HI_ON_ACT = (0, 2, 4, 6, 8, 10)
assert NC == len(MAXC) == 12

PREP = ["q0", "q1", "k0", "k1", "nq0", "nq1", "nk0", "nk1"]
USES = {
    "PRO": PREP + ["gate", "aug0", "aug1", "v0", "v1", "mb"],
    "FIRST": PREP + ["gate", "ma", "aug0", "aug1", "mx", "mgu", "v0", "v1", "mb", "meo"],
    "MID": PREP + ["pr0", "pr1", "gate", "ma", "aug0", "aug1", "mx", "mgu", "v0", "v1", "mb", "meo"],
    "LAST": ["pr0", "pr1", "ma", "mx", "mgu", "meo"],
    "FIN": ["pr0", "pr1"] + [f"ft{i}" for i in range(4)],
}
N_PRO, N_FIRST, N_MID, N_LAST = (len(USES[k]) for k in ("PRO", "FIRST", "MID", "LAST"))
assert N_PRO % 2 == 0 and N_FIRST % 2 == 0 and N_MID % 2 == 0 and N_LAST % 2 == 0


def use(kind, s, name):
    k = USES[kind].index(name)
    if kind == "PRO":
        base, half = 0, 0
    elif kind == "FIRST":
        base, half = N_PRO, N_PRO // 2
    elif kind == "MID":
        base = (s - 1) * N_MID + (N_PRO + N_FIRST)
        half = (s - 1) * (N_MID // 2) + (N_PRO + N_FIRST) // 2
    else:
        base = N_PRO + N_FIRST + (NPAIR - 2) * N_MID
        if kind == "FIN":
            base += N_LAST
        half = base // 2
    return k % 2, base + k + 1, half + k // 2


def wait(eng, sem, value):
    if isinstance(value, int) and value <= 0:
        return
    eng.wait_ge(sem, value)


def layer(nc, x, w3, wproj, qw, kw, om, u, gwt, gup, dwn, cst, augq, out):
    f32, r32, bf16, u32 = mybir.dt.float32, mybir.dt.float32r, mybir.dt.bfloat16, mybir.dt.uint32
    ALU, ACT, AX = mybir.AluOpType, mybir.ActivationFunctionType, mybir.AxisListType
    ctx = ExitStack()
    with ctx:
        def sb(name, shape, dt=f32):
            return ctx.enter_context(nc.sbuf_tensor(name, shape, dt))

        def sem(name):
            return ctx.enter_context(nc.semaphore(name))

        table = nc.dram_tensor("token_table", [NROWS, ROW], f32).ap()
        total = nc.dram_tensor("residual_and_experts", [NROWS, C], f32).ap()

        K = sb("consts", [P, K_END])
        ident = K[:, K_ID:K_ID + P]
        neg_p = K[:, K_NP:K_NP + 1]
        slot_no = K[:, K_SLOT:K_SLOT + P]
        blk_ones = K[:, K_ONES:K_ONES + P]
        head_of = K[:, K_UM:K_UM + 2]
        slopes = K[:, K_SL:K_SL + 2 * NPAIR]
        own_slot_no = K[:, K_OWN:K_OWN + CAP // 4]
        maskb = sb("mask_bf16", [P, 3 * P], bf16)
        ident_b, mask_qk, mask_kq = maskb[:, 0:P], maskb[:, P:2 * P], maskb[:, 2 * P:3 * P]
        qwk = sb("qk_norm_weights", [P, 3])
        omE = sb("minus_omega", [P, 3, 2 * NPAIR])
        uc = sb("u_columns", [P, 3, NPAIR])
        U2 = sb("u_pair", [P, 2, 2])
        eps = sb("eps", [P, 2])
        gw = sb("router_weight", [P, E])

        PR = sb("probs", [P, 4, CH])
        X = PR[:, :, :].rearrange("p a (t c) -> p (a t) c", c=C)
        ACC = sb("attn_out_T", [P, 3 * T])
        acc = ACC[:, 0:N]
        R = ACC[:, N:3 * T].rearrange("p (j r) -> p j r", r=P)
        XW = ACC[:, 0:NT * ROW].rearrange("p (t r) -> p t r", r=ROW)
        xh, xl = sb("xn_hi", [P, N], r32), sb("xn_lo", [P, N], r32)

        wraw = sb("w_raw", [P, 3 * P])
        wh, wl = sb("w_hi", [P, 3 * P], r32), sb("w_lo", [P, 3 * P], r32)
        RAW = sb("qk", [P, 2, T])
        SQ = sb("qk_sq", [P, 2, T])
        LO = SQ
        HIT = sb("qk_hi", [P, N + CAP], r32)
        HI = HIT[:, 0:N].rearrange("p (a t) -> p a t", a=2)
        vT = sb("vT", [P, T])
        GT = sb("gate_work", [P, 6, 2 * TB])
        QM, KM, QX, KX = ([sb(f"{n}{i}", [P, 2, T], r32) for i in range(2)] for n in ("QM", "KM", "QX", "KX"))
        VH, VL = ([sb(f"{n}{i}", [P, TB, 2, P], r32) for i in range(2)] for n in ("v_hi", "v_lo"))

        mx = sb("row_max_halves", [P, 4, 2])
        mcol = sb("row_max", [P, TB])
        mrow = sb("minus_max_row", [TB, 2, P], r32)
        PH, PL = sb("probs_hi", [P, 4, CH], r32), sb("probs_lo", [P, 4, CH], r32)
        RL = sb("inverse_sums", [D, T])
        Y = sb("y", [P, T])
        AQ = Y
        wp = sb("w_proj", [P, C])

        idxT = sb("slot_token", [P, E], u32)
        idxc = [sb(f"slot_token_pair{i}", [P, 2], u32) for i in range(2)]
        G = [sb(f"gathered{i}", [P, 2, ROW]) for i in range(2)]
        wgu = [sb(f"w_gate_up{i}", [P, 2, 2 * F]) for i in range(2)]
        wdn = [sb(f"w_down{i}", [F, 2, C]) for i in range(2)]
        XG = sb("gathered_T", [P, 2 * CAP])
        SGP = sb("silu_work", [P, 3, 2 * CAP])
        SG = SGP[0:F, :, :]
        YW = sb("expert_rows", [P, 2, C])

        xf = HIT[:, 0:N].bitcast(f32)
        CUM = HIT[:, :].bitcast(f32)
        prob = SQ[:, 0, 0:NT * E].rearrange("p (t e) -> p t e", e=E)
        repl = SQ[:, 0, NT * E:2 * NT * E].rearrange("p (t e) -> p t e", e=E)
        chosen = SQ[:, 1, 0:NT * E].rearrange("p (t e) -> p t e", e=E)
        selr = RAW[:, 0, :].bitcast(bf16)[:, 0:NT * P].rearrange("p (t g e) -> p t g e", g=4, e=E)
        masks = vT[:, CH:CH + 2 * P]
        ZR = vT[:, 0:ROW]
        stats = SGP[:, 0, 0:6 * NT].rearrange("p (t k) -> p t k", k=6)
        mv = SGP[:, 0, 6 * NT:8 * NT].rearrange("p (t k) -> p t k", k=2)
        rs = SGP[:, 0, 8 * NT:10 * NT].rearrange("p (k t) -> p k t", k=2)
        tops = SGP[:, 1, 0:NT * TOPK].rearrange("p (t k) -> p t k", k=TOPK)
        rsum = SGP[:, 2, 0:3 * NT].rearrange("p (k t) -> p k t", k=3)
        idx = SGP[:, 2, 3 * NT:3 * NT + E].bitcast(u32)
        ONES = RAW[:, 1, 0:CH]
        res = RAW[:, :, :].rearrange("p a (t c) -> p (a t) c", c=C)
        fin = SQ[:, :, :].rearrange("p a (t c) -> p (a t) c", c=C)

        SM = ctx.enter_context(nc.psum_tensor("SM", [P, 2, CH], f32))
        ST = ctx.enter_context(nc.psum_tensor("ST", [P, 2, CH], f32))
        AV = ctx.enter_context(nc.psum_tensor("AV", [P, T], f32))
        XB = ctx.enter_context(nc.psum_tensor("XB", [P, 2, CH], f32))

        S = {n: sem(n) for n in (
            "const_in", "x_in", "w_in", "wp_in", "we_in", "gather_in", "table_out", "total_out", "out_out",
            "consts_ready", "mask_ready", "stats_ready", "ln_var", "ln_rstd", "xn_ready", "zero_ready",
            "xt_psum", "xt_copied", "xh_ready", "xl_ready", "logit_psum", "logit_done", "selr_ready",
            "selT_psum", "selT_done", "idx_ready", "rt", "rt_exp", "omega_exp", "omega_ready", "u_sq",
            "u_psum", "u_ln", "u_ready", "rows_ready", "v_ones", "wts_ready", "pool_c", "pool_steps", "sp_steps",
            "spare_ready", "spare_free0", "spare_free1",
            "w_hi_ready", "w_lo_ready", "sq_ready", "rs_ln", "rs_ready", "qk_ready", "hi_ready",
            "lo_q_ready", "lo_k_ready", "spread_done", "v_hi_ready", "v_ready", "u2_ready", "gl_ready", "gate_abs", "gate_exp",
            "gate_ln", "gs", "bias_ready", "bias_rows_ready",
            "max_scores", "max_taken", "max_half", "max_ready", "mrow_ready", "mrow_in", "scores", "probs_ready", "hi_act", "hi_dve", "lo_probs",
            "pv_done", "sum_ln", "sum_inv", "y_ready", "proj_added",
            "idxc_ready", "xg_ready", "sg_exp", "sg", "h_ready", "yw_ready", "scatter_done", "final_ready", "res_in")}
        spare_free = [S["spare_free0"], S["spare_free1"]]
        block = ctx.enter_context(nc.Block())

        SPREAD = 12

        def hi_ready(n, i):
            mine = [k for k in range(NC) if (k in HI_ON_ACT) == (i in HI_ON_ACT)]
            return S["hi_act" if i in HI_ON_ACT else "hi_dve"], len(mine) * n + (mine.index(i) + 1)

        def batch(s):
            return s // (H // 2)

        def pair(s):
            return s % (H // 2)

        @block.sync
        def _(sp):
            sp.dma_start(X[:, :, :], x.rearrange("(t p) c -> p t c", p=P)).then_inc(S["x_in"], 16)
            for dst, src in ((K[:, :], cst[:, 0:K_END]), (masks, cst[:, K_END:K_ALL]), (AQ[:, :], augq), (qwk[:, 0:1], qw), (qwk[:, 1:2], kw),
                             (omE[:, 0, :], om), (uc[:, 0, :], u), (gw[:, :], gwt)):
                sp.dma_start(dst, src).then_inc(S["const_in"], 16)

            def stand(value):
                if not isinstance(value, int):
                    sp.sem_inc(S["sp_steps"], 1)

            def load_w(s, wait_for):
                if wait_for is not None:
                    wait(sp, S["w_hi_ready"], wait_for)
                    wait(sp, S["w_lo_ready"], wait_for)
                sp.dma_start(wraw[:, :], w3[bass.ds(pair(s), 1), :, :].rearrange("a p n -> (a p) n")
                             ).then_inc(S["w_in"], 16)

            def spread(s, b):
                wait(sp, S["pv_done"], NC * (2 * s - 2))
                stand(s)
                for t in (0, 1):
                    sp.wait_ge(S["hi_ready"], 2 * s + t + 1)
                    main, cross = ((QM, QX), (KM, KX))[t]
                    for a in range(2):
                        src = HI[D * a:D * a + D, t, :].bitcast(f32)
                        sp.dma_start(main[b][0:D, a, :].bitcast(f32), src).then_inc(S["spread_done"], 16)
                        sp.dma_start(cross[b][D * (1 - t):D * (2 - t), a, :].bitcast(f32), src).then_inc(S["spread_done"], 16)
                    sp.wait_ge(S[("lo_q_ready", "lo_k_ready")[t]], s + 1)
                    for a in range(2):
                        sp.dma_start(cross[b][D * t:D * t + D, a, :].bitcast(f32), LO[D * a:D * a + D, t, :]
                                     ).then_inc(S["spread_done"], 16)

            def load_experts(s, b):
                if not isinstance(s, int) or s >= 2:
                    sp.wait_ge(S["yw_ready"], s - 1)
                sp.dma_start(wgu[b][:, :, :], gup[bass.ds(s, 1), :, :].rearrange("a p (e n) -> (a p) e n", e=2)
                             ).then_inc(S["we_in"], 16)
                sp.dma_start(wdn[b][:, :, :], dwn[bass.ds(s, 1), :, :].rearrange("a p (e n) -> (a p) e n", e=2)
                             ).then_inc(S["we_in"], 16)

            load_w(0, None)
            sp.wait_ge(S["zero_ready"], 1)
            sp.dma_start(table[N:NROWS, :], ZR[:, :]).then_inc(S["table_out"], 16)
            sp.dma_start(total[N:NROWS, :], ZR[:, 0:C]).then_inc(S["total_out"], 16)
            sp.wait_ge(S["x_in"], 16)
            sp.dma_start(total[0:N, :].rearrange("(t p) c -> p t c", p=P), X[:, :, :]).then_inc(S["total_out"], 16)
            sp.wait_ge(S["wts_ready"], 1)
            sp.dma_start(table[0:N, :].rearrange("(t p) c -> p t c", p=P), XW[:, :, :]).then_inc(S["table_out"], 16)
            load_w(1, 1)
            spread(0, 0)

            def period(s, b, kind):
                if kind != "LAST":
                    load_w(s + 2, s + 2)
                load_experts(s, b)
                if kind != "LAST":
                    spread(s + 1, 1 - b)
                if kind != "FIRST":
                    _, ready, _ = use(kind, s, "pr1")
                    sp.wait_ge(S["spare_ready"], ready)
                sp.dma_start(wp[:, :], wproj[bass.ds(pair(s), 1), :, :].rearrange("a p n -> (a p) n")
                             ).then_inc(S["wp_in"], 16)

            period(0, 0, "FIRST")
            with sp.Fori(0, (NPAIR - 2) // 2) as it:
                period(2 * it + 1, 1, "MID")
                period(2 * it + 2, 0, "MID")
            period(NPAIR - 1, 1, "LAST")
            sp.wait_ge(S["scatter_done"], 32 * NPAIR)
            sp.dma_start(res, total[0:N, :].rearrange("(t p) c -> p t c", p=P)).then_inc(S["res_in"], 16)
            for g in range(4):
                sp.wait_ge(S["final_ready"], g + 1)
                sp.dma_start(out[g * CH:(g + 1) * CH, :].rearrange("(t p) c -> p t c", p=P),
                             fin[:, 4 * g:4 * g + 4, :]).then_inc(S["out_out"], 16)
            sp.wait_ge(S["out_out"], 64)
            sp.wait_ge(S["table_out"], 32)
            sp.wait_ge(S["total_out"], 32)

        @block.tensor
        def _(pe):
            mm = nc.tensor.matmul

            def mm3(o, whi, wlo, xhi, xlo):
                mm(o, wlo, xhi, start=True, stop=False)
                mm(o, whi, xlo, start=False, stop=False)
                return mm(o, whi, xhi, start=False, stop=True)

            def spare(kind, s, name):
                bank, ready, earlier = use(kind, s, name)
                wait(pe, spare_free[bank], earlier)
                return XB[:, bank, :]

            def project(kind, s, name, bt):
                o = spare(kind, s, name)
                i, c = "qk".index(name[0]), int(name[1])
                w, tokens = slice(i * P, (i + 1) * P), slice(bt * T + c * CH, bt * T + (c + 1) * CH)
                mm3(o, wh[:, w], wl[:, w], xh[:, tokens], xl[:, tokens]).then_inc(S["spare_ready"], 1)

            def values(kind, s, name, bt):
                o = spare(kind, s, name)
                for j in range(4):
                    block = slice(bt * T + int(name[1]) * CH + j * P, bt * T + int(name[1]) * CH + (j + 1) * P)
                    last = mm3(o[:, j * P:(j + 1) * P], xh[:, block], xl[:, block], wh[:, 2 * P:], wl[:, 2 * P:])
                last.then_inc(S["spare_ready"], 1)

            def head_norm(kind, s, name):
                o = spare(kind, s, name)
                t, c = "qk".index(name[1]), int(name[2])
                mm(o, blk_ones, SQ[:, t, c * CH:(c + 1) * CH], start=True, stop=True).then_inc(S["spare_ready"], 1)

            def gate(kind, s):
                o = spare(kind, s, "gate")
                for j in range(TB):
                    last = mm(o[:, 2 * j:2 * j + 2], RAW[:, 1, j * P:(j + 1) * P], U2[:, 0, :], start=True, stop=True)
                last.then_inc(S["spare_ready"], 1)

            def bias_rows(kind, s, name):
                o = spare(kind, s, name)
                c = int(name[3])
                for j in range(4):
                    last = nc.tensor.transpose(o[:, j * P:(j + 1) * P], R[:, 4 * c + j, :], ident)
                last.then_inc(S["spare_ready"], 1)

            def prep(kind, s, p, bt, step):
                if step == 0:
                    pe.wait_ge(S["w_hi_ready"], p + 1)
                    pe.wait_ge(S["w_lo_ready"], p + 1)
                    for n in ("q0", "q1"):
                        project(kind, s, n, bt)
                elif step == 2:
                    for n in ("k0", "k1"):
                        project(kind, s, n, bt)
                elif step == 4:
                    pe.wait_ge(S["sq_ready"], 4 * p + 2)
                    for n in ("nq0", "nq1"):
                        head_norm(kind, s, n)
                elif step == 6:
                    pe.wait_ge(S["sq_ready"], 4 * p + 4)
                    for n in ("nk0", "nk1"):
                        head_norm(kind, s, n)
                elif step == 9:
                    pe.wait_ge(S["qk_ready"], 2 * p + 2)
                    pe.wait_ge(S["u2_ready"], p + 1)
                    gate(kind, s)
                elif step == 11:
                    pe.wait_ge(S["bias_ready"], p + 1)
                    for n in ("aug0", "aug1"):
                        bias_rows(kind, s, n)

            def prep_values(kind, s, bt, step):
                if step == 6:
                    for n in ("v0", "v1"):
                        values(kind, s, n, bt)

            def max_chunk(n, b, a, i):
                ib, j0, w, diag = MAXC[i]
                wait(pe, S["max_taken"], NC * n + i - 1)
                o = SM[:, i % 2, 0:w]
                last = mm(o, QM[b][0:MROW, a, ib * P:(ib + 1) * P], KM[b][0:MROW, a, j0:j0 + w],
                          start=True, stop=not diag)
                if diag:
                    last = mm(SM[:, i % 2, w - P:w], ident_b, mask_qk, start=False, stop=True)
                last.then_inc(S["max_scores"], 1)

            def max_row(kind, s, name, n):
                o = spare(kind, s, name)
                pe.wait_ge(S["max_ready"], n + 1)
                nc.tensor.transpose(o[0:TB, 0:P], mcol[:, :], ident).then_inc(S["spare_ready"], 1)

            def score_chunk(n, b, a, i):
                jb, c, q0, w, diag = STC[i]
                wait(pe, S["probs_ready"], NC * n + i - 1)
                o = ST[:, i % 2, 0:w]
                keys = slice(jb * P, (jb + 1) * P)
                mm(o, KX[b][:, a, keys], QX[b][:, a, q0:q0 + w], start=True, stop=False)
                last = mm(o, KM[b][0:MROW + 1, a, keys], QM[b][0:MROW + 1, a, q0:q0 + w], start=False, stop=not diag)
                if diag:
                    last = mm(ST[:, i % 2, 0:P], ident_b, mask_kq, start=False, stop=True)
                last.then_inc(S["scores"], 1)

            def moe_step(kind, s, b, step):
                if step == 1:
                    pe.wait_ge(S["gather_in"], 32 * (s + 1))
                    o = spare(kind, s, "mx")
                    for e in range(2):
                        last = nc.tensor.transpose(o[:, e * P:(e + 1) * P], G[b][:, e, 0:C], ident)
                    last.then_inc(S["spare_ready"], 1)
                elif step == 3:
                    pe.wait_ge(S["xg_ready"], s + 1)
                    pe.wait_ge(S["we_in"], 32 * (s + 1))
                    o = spare(kind, s, "mgu")
                    for gu in range(2):
                        for e in range(2):
                            at = gu * 2 * CAP + e * CAP
                            last = mm(o[0:F, at:at + CAP], wgu[b][:, e, gu * F:(gu + 1) * F],
                                      XG[:, e * CAP:(e + 1) * CAP], start=True, stop=True)
                    last.then_inc(S["spare_ready"], 1)
                elif step == 10:
                    pe.wait_ge(S["h_ready"], s + 1)
                    o = spare(kind, s, "meo")
                    for e in range(2):
                        last = mm(o[:, e * C:(e + 1) * C], SG[:, 2, e * CAP:(e + 1) * CAP], wdn[b][:, e, :],
                                  start=True, stop=True)
                    last.then_inc(S["spare_ready"], 1)

            def project_out(kind, s, p):
                pe.wait_ge(S["y_ready"], 4 * p + 4)
                pe.wait_ge(S["wp_in"], 16 * (p + 1))
                for c in range(2):
                    o = spare(kind, s, f"pr{c}")
                    mm(o, wp[:, :], Y[:, c * CH:(c + 1) * CH], start=True, stop=True).then_inc(S["spare_ready"], 1)

            pe.wait_ge(S["consts_ready"], 1)
            pe.wait_ge(S["u_sq"], 1)
            mm(AV[:, 0:NPAIR], blk_ones, uc[:, 1, :], start=True, stop=True).then_inc(S["u_psum"], 1)
            for g in range(4):
                pe.wait_ge(S["xn_ready"], g + 1)
                wait(pe, S["xt_copied"], g - 1)
                for j in range(4):
                    last = nc.tensor.transpose(ST[:, g % 2, j * P:(j + 1) * P], XW[:, 4 * g + j, 0:C], ident)
                last.then_inc(S["xt_psum"], 1)
            for t in range(NT):
                if t % 4 == 0:
                    pe.wait_ge(S["xt_copied"], t // 4 + 1)
                last = mm(SM[:, 0, t * E:(t + 1) * E], xf[:, t * P:(t + 1) * P], gw[:, :], start=True, stop=True)
            last.then_inc(S["logit_psum"], 1)
            pe.wait_ge(S["selr_ready"], 1)
            pe.wait_ge(S["mask_ready"], 1)
            for g in range(4):
                if g >= 2:
                    pe.wait_ge(S["selT_done"], g - 1)
                for j in range(4):
                    last = mm(ST[:, g % 2, j * P:(j + 1) * P],
                              selr[:, 4 * g + j, :, :].rearrange("p g e -> p (g e)"), ident_b, start=True, stop=True)
                last.then_inc(S["selT_psum"], 1)
            pe.wait_ge(S["selT_done"], 4)
            pe.wait_ge(S["xh_ready"], 4)
            pe.wait_ge(S["xl_ready"], 4)
            pe.wait_ge(S["u_ready"], 1)
            for step in range(NC):
                prep("PRO", 0, 0, 0, step)
            for step in range(NC):
                prep_values("PRO", 0, 0, step)

            def first_use(p, with_rows):
                pe.wait_ge(S["spread_done"], 16 * SPREAD * (p + 1))
                pe.wait_ge(S["bias_rows_ready"], 4 * (p + 1))
                if with_rows:
                    pe.wait_ge(S["rows_ready"], 8)

            first_use(0, True)
            for i in range(NC):
                max_chunk(0, 0, 0, i)
            max_row("PRO", 0, "mb", 0)

            def values_product(n, b, a, k):
                jb, c, q0, w, _ = STC[k]
                if k == 0 and a == 0:
                    pe.wait_ge(S["v_ready"], n + 2)
                if jb == 0:
                    wait(pe, S["y_ready"], 2 * n - 1 + c)
                o = AV[:, q0:q0 + w]
                hi_made, count = hi_ready(n, k)
                pe.wait_ge(hi_made, count)
                mm(o, VL[b][:, jb, a, :], PH[:, k % 4, 0:w], start=(jb == 0), stop=False)
                mm(o, VH[b][:, jb, a, :], PH[:, k % 4, 0:w], start=False, stop=False)
                pe.wait_ge(S["lo_probs"], NC * n + k + 1)
                mm(o, VH[b][:, jb, a, :], PL[:, k % 4, 0:w], start=False, stop=(jb == 4 * c + 3)
                   ).then_inc(S["pv_done"], 1)

            def slot(s, b, a, kind, bt, nxt):
                n = 2 * s + a
                nb = b if a == 0 else 1 - b
                pe.wait_ge(S["mrow_in"], 16 * (n + 1))
                first = FIRST_MAX[a]
                for i in range(NC):
                    score_chunk(n, b, a, i)
                    if nxt and first <= i < first + 6:
                        if i == first and a == 1:
                            first_use(s + 1, False)
                        for k in (2 * (i - first), 2 * (i - first) + 1):
                            max_chunk(n + 1, nb, 1 - a, k)
                    if a == 0 and kind != "LAST":
                        prep(kind, s, s + 1, bt, i)
                    if a == 0 and i == 8 and kind != "FIRST":
                        project_out(kind, s, s - 1)
                    if a == 1 and kind != "LAST":
                        prep_values(kind, s, bt, i)
                    if i == MAX_ROW[a] and nxt:
                        max_row(kind, s, "ma" if a == 0 else "mb", n + 1)
                    if a == 1:
                        moe_step(kind, s, b, i)
                    if i >= LAG:
                        values_product(n, b, a, i - LAG)
                    elif not (kind == "FIRST" and a == 0):
                        values_product(n - 1, 1 - b if a == 0 else b, 1 - a, NC + i - LAG)

            def period(s, b, kind, bt):
                slot(s, b, 0, kind, bt, True)
                slot(s, b, 1, kind, bt, kind != "LAST")

            pe.wait_ge(S["v_ones"], 1)
            period(0, 0, "FIRST", 0)
            with pe.Fori(0, (NPAIR // 2 - 2) // 2) as it:
                period(2 * it + 1, 1, "MID", 0)
                period(2 * it + 2, 0, "MID", 0)
            with pe.Fori(0, NPAIR // 4) as it:
                period(2 * it + (NPAIR // 2 - 1), 1, "MID", 1)
                period(2 * it + NPAIR // 2, 0, "MID", 1)
            period(NPAIR - 1, 1, "LAST", 1)
            for k in range(NC - LAG, NC):
                values_product(2 * NPAIR - 1, 1, 1, k)
            project_out("FIN", 0, NPAIR - 1)
            pe.wait_ge(S["proj_added"], 2 * NPAIR)
            for g in range(4):
                o = spare("FIN", 0, f"ft{g}")
                for j in range(4):
                    t = 4 * g + j
                    last = nc.tensor.transpose(o[:, j * P:(j + 1) * P], acc[:, t * P:(t + 1) * P], ident)
                last.then_inc(S["spare_ready"], 1)

        @block.scalar
        def _(act):
            fn = nc.scalar.activation

            def taken(kind, s, name):
                bank, ready, _ = use(kind, s, name)
                act.wait_ge(S["spare_ready"], ready)
                return XB[:, bank, :], spare_free[bank]

            def split_weights(p):
                act.wait_ge(S["w_in"], 16 * (p + 1))
                fn(wh[:, :], wraw[:, :], ACT.Copy).then_inc(S["w_hi_ready"], 1)

            def prep(kind, s, p, pb, step):
                if step in (1, 3):
                    t = (step - 1) // 2
                    wait(act, S[("lo_q_ready", "lo_k_ready")[t]], p)
                    wait(act, S["spread_done"], 16 * SPREAD * p)
                    for c in range(2):
                        o, free = taken(kind, s, f"{'qk'[t]}{c}")
                        half = slice(c * CH, (c + 1) * CH)
                        fn(RAW[:, t, half], o, ACT.Copy)
                        fn(SQ[:, t, half], o, ACT.Square).then_inc(S["sq_ready"], 1)
                        act.wait_ge(S["sq_ready"], 4 * p + 2 * t + c + 1)
                        act.sem_inc(free, 1)
                elif step in (5, 7):
                    t = (step - 5) // 2
                    for c in range(2):
                        o, free = taken(kind, s, f"n{'qk'[t]}{c}")
                        fn(SQ[:, t, c * CH:(c + 1) * CH], o, ACT.Ln, bias=eps[:, 0:1]).then_inc(free, 1)
                        act.wait_ge(free, use(kind, s, f"n{'qk'[t]}{c}")[2] + 1)
                    fn(SQ[:, t, :], SQ[:, t, :], ACT.Exp, scale=-0.5).then_inc(S["rs_ready"], 1)
                if step in (7, 9):
                    t = (step - 7) // 2
                    act.wait_ge(S["qk_ready"], 2 * p + t + 1)
                    wait(act, S["spread_done"], 16 * SPREAD * p)
                    fn(HI[:, t, :], RAW[:, t, :], ACT.Copy).then_inc(S["hi_ready"], 1)
                elif step == 10:
                    act.wait_ge(S["gl_ready"], p + 1)
                    fn(GT[:, 1, :], GT[:, 0, :], ACT.Abs).then_inc(S["gate_abs"], 1)
                    act.wait_ge(S["gate_abs"], p + 1)
                    fn(GT[:, 2, :], GT[:, 1, :], ACT.Exp, scale=-1.0).then_inc(S["gate_exp"], 1)
                    act.wait_ge(S["gate_exp"], p + 1)
                    fn(GT[:, 1, :], GT[:, 2, :], ACT.Ln, bias=1.0).then_inc(S["gate_ln"], 1)

            def prep_values(kind, s, p, pb, step):
                if step == 0:
                    wait(act, S["pv_done"], NC * (2 * p - 2))
                    for c in range(2):
                        o, free = taken(kind, s, f"aug{c}")
                        for a in range(2):
                            fn(KM[pb][AUG:AUG + 32, a, c * CH:(c + 1) * CH], o[AUG + 32 * a:AUG + 32 * a + 32, :],
                               ACT.Copy).then_inc(S["bias_rows_ready"], 1)
                        act.wait_ge(S["bias_rows_ready"], 4 * p + 2 * c + 2)
                        act.sem_inc(free, 1)
                elif step == 7:
                    for c in range(2):
                        o, _ = taken(kind, s, f"v{c}")
                        fn(VH[pb][:, 4 * c:4 * c + 4, :, 0:D], o.rearrange("p (j a d) -> p j a d", j=4, a=2),
                           ACT.Copy).then_inc(S["v_hi_ready"], 1)
                elif step == 8:
                    split_weights(p + 1)

            def max_row(kind, s, name, n, b, a, par):
                o, free = taken(kind, s, name)
                wait(act, S["mrow_in"], 16 * (n - 1))
                fn(mrow[:, par, :], o[0:TB, 0:P], ACT.Copy, scale=-1.0).then_inc(S["mrow_ready"], 1)
                act.wait_ge(S["mrow_ready"], n + 1)
                act.sem_inc(free, 1)
                act.dma_start(QM[b][MROW:MROW + 1, a, :].rearrange("o (k q) -> o k q", q=P).bitcast(f32),
                              mrow[:, par, :].bitcast(f32)).then_inc(S["mrow_in"], 16)

            def inverse_sums(n, c):
                act.wait_ge(S["pv_done"], NC * n + (HALF_DONE + 1 if c == 0 else NC))
                wait(act, S["y_ready"], 2 * n - 1 + c)
                half = RL[:, c * CH:(c + 1) * CH]
                fn(half, AV[D:2 * D, c * CH:(c + 1) * CH], ACT.Ln).then_inc(S["sum_ln"], 1)
                act.wait_ge(S["sum_ln"], 2 * n + c + 1)
                fn(half, half, ACT.Exp, scale=-1.0).then_inc(S["sum_inv"], 1)

            def moe_step(kind, s, step):
                if step == 2:
                    o, free = taken(kind, s, "mx")
                    fn(XG[:, :], o[:, 0:2 * CAP], ACT.Copy).then_inc(S["xg_ready"], 1)
                    act.wait_ge(S["xg_ready"], s + 1)
                    act.sem_inc(free, 1)
                elif step == 4:
                    bank, ready, _ = use(kind, s, "mgu")
                    act.wait_ge(S["spare_ready"], ready)
                    fn(SG[:, 0, :], XB[0:F, bank, 0:2 * CAP], ACT.Exp, scale=-1.0).then_inc(S["sg_exp"], 1)
                    act.wait_ge(S["sg_exp"], 3 * s + 1)
                    fn(SG[:, 1, :], SG[:, 0, :], ACT.Ln, bias=1.0).then_inc(S["sg_exp"], 1)
                    act.wait_ge(S["sg_exp"], 3 * s + 2)
                    fn(SG[:, 0, :], SG[:, 1, :], ACT.Exp, scale=-1.0).then_inc(S["sg_exp"], 1)

            act.preload_act_table_set("natural_log_exp_and_others")
            act.wait_ge(S["const_in"], 16 * 8)
            act.wait_ge(S["pool_c"], 2)
            fn(omE[:, 1, :], omE[:, 0, :], ACT.Abs).then_inc(S["omega_exp"], 1)
            act.wait_ge(S["omega_exp"], 1)
            fn(omE[:, 2, :], omE[:, 1, :], ACT.Exp, scale=-1.0).then_inc(S["omega_exp"], 1)
            act.wait_ge(S["omega_exp"], 2)
            fn(omE[:, 1, :], omE[:, 2, :], ACT.Ln, bias=1.0).then_inc(S["omega_exp"], 1)
            act.wait_ge(S["ln_var"], NT)
            fn(rs[:, 0, :], mv[:, :, 1], ACT.Ln, bias=eps[:, 0:1]).then_inc(S["ln_rstd"], 1)
            act.wait_ge(S["ln_rstd"], 1)
            fn(rs[:, 1, :], rs[:, 0, :], ACT.Exp, scale=-0.5).then_inc(S["ln_rstd"], 1)
            act.wait_ge(S["u_ln"], 1)
            fn(uc[:, 2, :], uc[:, 1, :], ACT.Ln).then_inc(S["u_ln"], 1)
            act.wait_ge(S["u_ln"], 2)
            fn(uc[:, 1, :], uc[:, 2, :], ACT.Exp, scale=-0.5).then_inc(S["u_ln"], 1)
            for g in range(4):
                act.wait_ge(S["xt_copied"], g + 1)
                fn(xh[:, g * CH:(g + 1) * CH], xf[:, g * CH:(g + 1) * CH], ACT.Copy).then_inc(S["xh_ready"], 1)
            act.wait_ge(S["rt_exp"], 1)
            fn(prob, chosen, ACT.Exp).then_inc(S["rt_exp"], 1)
            act.wait_ge(S["idx_ready"], 1)
            act.wait_ge(S["xl_ready"], 4)
            act.wait_ge(S["total_out"], 32)
            act.wait_ge(S["table_out"], 32)
            split_weights(0)
            for step in range(NC):
                prep("PRO", 0, 0, 0, step)
            for step in range(NC):
                prep_values("PRO", 0, 0, 0, step)
            max_row("PRO", 0, "mb", 0, 0, 0, 0)

            def slot(s, b, a, kind, nxt):
                n = 2 * s + a
                for i in range(NC):
                    jb, c, q0, w, _ = STC[i]
                    act.wait_ge(S["scores"], NC * n + i + 1)
                    wait(act, S["lo_probs"], NC * n + i - 3)
                    if i in HI_ON_ACT:
                        wait(act, S["pv_done"], NC * n + i - 3)
                        fn(PH[:, i % 4, 0:w], ST[:, i % 2, 0:w], ACT.Exp).then_inc(S["hi_act"], 1)
                    fn(PR[:, i % 4, 0:w], ST[:, i % 2, 0:w], ACT.Exp).then_inc(S["probs_ready"], 1)
                    if i == SUMS[1] and not (kind == "FIRST" and a == 0):
                        inverse_sums(n - 1, 1)
                    if i == SUMS[0]:
                        inverse_sums(n, 0)
                    if a == 0 and kind != "LAST":
                        prep(kind, s, s + 1, 1 - b, i)
                    if a == 1:
                        moe_step(kind, s, i)
                        if kind != "LAST":
                            prep_values(kind, s, s + 1, 1 - b, i)
                    if i == MAX_ROW[a] and nxt:
                        nb = b if a == 0 else 1 - b
                        max_row(kind, s, "ma" if a == 0 else "mb", n + 1, nb, 1 - a, 1 - a)

            def period(s, b, kind):
                slot(s, b, 0, kind, True)
                slot(s, b, 1, kind, kind != "LAST")

            period(0, 0, "FIRST")
            with act.Fori(0, (NPAIR - 2) // 2) as it:
                period(2 * it + 1, 1, "MID")
                period(2 * it + 2, 0, "MID")
            period(NPAIR - 1, 1, "LAST")
            inverse_sums(2 * NPAIR - 1, 1)

        @block.vector
        def _(dve):
            v = nc.vector

            def taken(kind, s, name):
                bank, ready, _ = use(kind, s, name)
                dve.wait_ge(S["spare_ready"], ready)
                return XB[:, bank, :], spare_free[bank]

            def diag(row0):
                return bass.AP(ACC[:, :].tensor, N + AUG + row0, [[3 * T, P], [P + 1, TB], [32, 2]])

            def gate_bias(p):
                def step(k):
                    return GS * p + k
                GS = 4
                dve.wait_ge(S["gate_ln"], p + 1)
                v.scalar_tensor_tensor(GT[:, 3, :], GT[:, 0, :], 0.0, GT[:, 1, :], op0=ALU.max, op1=ALU.add
                                       ).then_inc(S["gs"], 1)
                dve.wait_ge(S["gs"], step(1))
                v.tensor_tensor(GT[:, 4, :].rearrange("p (j a) -> p j a", a=2),
                                GT[:, 3, :].rearrange("p (j a) -> p j a", a=2),
                                omE[:, 0, bass.ds(2 * p, 2)].unsqueeze(1).to_broadcast([P, TB, 2]), ALU.mult
                                ).then_inc(S["gs"], 1)
                dve.wait_ge(S["gs"], step(2))
                g3 = GT[:, 4, :].rearrange("p (j a) -> p j a", a=2)
                j3 = GT[:, 5, :].rearrange("p (j a) -> p j a", a=2)
                v.tensor_scalar(GT[:, 5, :], GT[:, 4, :], neg_p, None, ALU.mult).then_inc(S["gs"], 1)
                v.tensor_copy(diag(0).bitcast(r32), g3)
                dve.wait_ge(S["gs"], step(3))
                Rv = R[:, :, AUG:AUG + 64].rearrange("p j (a r) -> p j a r", a=2)
                v.tensor_copy(Rv[:, :, :, 16].bitcast(r32), j3).then_inc(S["gs"], 1)
                dve.wait_ge(S["gs"], step(4))
                v.tensor_tensor(diag(8), g3, diag(0), ALU.subtract)
                v.tensor_tensor(Rv[:, :, :, 17], j3, Rv[:, :, :, 16], ALU.subtract).then_inc(S["bias_ready"], 1)

            def split_weights(p):
                dve.wait_ge(S["w_hi_ready"], p + 1)
                v.tensor_tensor(wl[:, :], wraw[:, :], wh[:, :].bitcast(f32), ALU.subtract
                                ).then_inc(S["w_lo_ready"], 1)

            def prep(kind, s, p, pb, step):
                if step == 0:
                    v.tensor_scalar(U2[:, 0, :], head_of, uc[:, 0, bass.ds(p, 1)], None, ALU.mult
                                    ).then_inc(S["u2_ready"], 1)
                elif step in (6, 8):
                    t = (step - 6) // 2
                    dve.wait_ge(S["rs_ready"], 2 * p + t + 1)
                    v.scalar_tensor_tensor(RAW[:, t, :], RAW[:, t, :], qwk[:, 2 - t:3 - t], SQ[:, t, :],
                                           op0=ALU.mult, op1=ALU.mult).then_inc(S["qk_ready"], 1)
                elif step == 9:
                    o, free = taken(kind, s, "gate")
                    v.tensor_copy(GT[:, 0, :], o[:, 0:2 * TB]).then_inc(S["gl_ready"], 1)
                    dve.wait_ge(S["gl_ready"], p + 1)
                    dve.sem_inc(free, 1)
                elif step == 10:
                    gate_bias(p)

            def prep_values(kind, s, p, pb, step):
                if step == 7:
                    for c in range(2):
                        o, free = taken(kind, s, f"v{c}")
                        dve.wait_ge(S["v_hi_ready"], 2 * p + c + 1)
                        blocks = slice(4 * c, 4 * c + 4)
                        v.tensor_tensor(VL[pb][:, blocks, :, 0:D], o.rearrange("p (j a d) -> p j a d", j=4, a=2),
                                        VH[pb][:, blocks, :, 0:D].bitcast(f32), ALU.subtract
                                        ).then_inc(S["v_ready"], 1)
                        dve.wait_ge(S["v_ready"], 2 * p + c + 1)
                        dve.sem_inc(free, 1)
                elif step == 8:
                    split_weights(p + 1)

            def max_chunk(n, i):
                ib, j0, w, _ = MAXC[i]
                dve.wait_ge(S["max_scores"], NC * n + i + 1)
                o = mcol[:, ib:ib + 1] if ib < 4 else mx[:, ib - 4, j0 // CH:j0 // CH + 1]
                if i == 0:
                    wait(dve, S["mrow_ready"], n)
                last = v.tensor_reduce(o, SM[:, i % 2, 0:w], axis=AX.X, op=ALU.max).then_inc(S["max_taken"], 1)
                if i == NC - 1:
                    dve.wait_ge(S["max_taken"], NC * (n + 1))
                    v.tensor_tensor(mcol[:, 4:8], mx[:, :, 0], mx[:, :, 1], ALU.max).then_inc(S["max_ready"], 1)

            def split_probs(n, i):
                w = STC[i][3]
                hi, lo, both = PH[:, i % 4, 0:w], PL[:, i % 4, 0:w], PR[:, i % 4, 0:w]
                wait(dve, S["pv_done"], NC * n + i - 3)
                dve.wait_ge(S["probs_ready"], NC * n + i + 1)
                hi_made, count = hi_ready(n, i)
                if i not in HI_ON_ACT:
                    v.tensor_copy(hi, both).then_inc(hi_made, 1)
                dve.wait_ge(hi_made, count)
                v.tensor_tensor(lo, both, hi.bitcast(f32), ALU.subtract).then_inc(S["lo_probs"], 1)

            def normalise(n, a, p, c):
                dve.wait_ge(S["sum_inv"], 2 * n + c + 1)
                if a == 0:
                    wait(dve, S["proj_added"], 2 * p)
                half = slice(c * CH, (c + 1) * CH)
                v.tensor_tensor(Y[D * a:D * a + D, half], AV[0:D, half], RL[:, half], ALU.mult
                                ).then_inc(S["y_ready"], 1)

            def add_projection(kind, s, p):
                for c in range(2):
                    o, free = taken(kind, s, f"pr{c}")
                    dst = acc[:, bass.ds(batch(p) * T + c * CH, CH)]
                    v.tensor_tensor(dst, o, dst, ALU.add).then_inc(S["proj_added"], 1)
                    dve.wait_ge(S["proj_added"], 2 * p + c + 1)
                    dve.sem_inc(free, 1)

            def moe_step(kind, s, b, step):
                if step == 5:
                    bank, ready, _ = use(kind, s, "mgu")
                    up = XB[0:F, bank, 2 * CAP:4 * CAP]
                    gt = XB[0:F, bank, 0:2 * CAP]
                    dve.wait_ge(S["sg_exp"], 3 * s + 3)
                    v.tensor_tensor(SG[:, 1, :], gt, SG[:, 0, :], ALU.mult).then_inc(S["sg"], 1)
                    dve.wait_ge(S["sg"], s + 1)
                    v.tensor_tensor(SG[:, 2, :], up, SG[:, 1, :], ALU.mult).then_inc(S["h_ready"], 1)
                    dve.wait_ge(S["h_ready"], s + 1)
                    dve.sem_inc(spare_free[bank], 1)
                elif step == 11:
                    o, free = taken(kind, s, "meo")
                    wait(dve, S["scatter_done"], 32 * s)
                    for e in range(2):
                        last = v.tensor_scalar(YW[:, e, :], o[:, e * C:(e + 1) * C],
                                               G[b][:, e, bass.ds(2 * s + (C + e), 1)], None, ALU.mult)
                    last.then_inc(S["yw_ready"], 1)
                    dve.wait_ge(S["yw_ready"], s + 1)
                    dve.sem_inc(free, 1)

            count = [0]

            def rt(ins):
                count[0] += 1
                ins.then_inc(S["rt"], 1)
                dve.wait_ge(S["rt"], count[0])

            dve.wait_ge(S["x_in"], 16)
            for t in range(NT):
                v.bn_stats(stats[:, t, :], X[:, t, :]).then_inc(S["stats_ready"], 1)
            dve.wait_ge(S["stats_ready"], NT)
            for t in range(NT):
                v.bn_aggr(mv[:, t, :], stats[:, t, :]).then_inc(S["ln_var"], 1)
            dve.wait_ge(S["const_in"], 16 * 8)
            v.tensor_copy(maskb[:, 0:P], ident)
            v.tensor_copy(maskb[:, P:3 * P], masks).then_inc(S["mask_ready"], 1)
            rt(v.tensor_tensor(uc[:, 1, :], uc[:, 0, :], uc[:, 0, :], ALU.mult))
            dve.sem_inc(S["u_sq"], 1)
            dve.sem_inc(S["consts_ready"], 1)
            rt(v.tensor_scalar(qwk[:, 2:3], qwk[:, 0:1], 0.125, None, ALU.mult))
            dve.wait_ge(S["ln_rstd"], 2)
            dve.wait_ge(S["ln_var"], NT)
            for t in range(NT):
                last = v.tensor_scalar(XW[:, t, 0:C], X[:, t, :], mv[:, t, 0:1], rs[:, 1, t:t + 1],
                                       ALU.subtract, ALU.mult)
                if t % 4 == 3:
                    last.then_inc(S["xn_ready"], 1)
            dve.wait_ge(S["u_psum"], 1)
            v.tensor_scalar(uc[:, 1, :], AV[:, 0:NPAIR], float(D), 1e-12, ALU.mult, ALU.max).then_inc(S["u_ln"], 1)
            for g in range(4):
                dve.wait_ge(S["xt_psum"], g + 1)
                v.tensor_copy(xf[:, g * CH:(g + 1) * CH], ST[:, g % 2, :]).then_inc(S["xt_copied"], 1)
            dve.wait_ge(S["u_ln"], 3)
            rt(v.tensor_scalar(uc[:, 1, :], uc[:, 1, :], 0.125, None, ALU.mult))
            v.tensor_tensor(uc[:, 0, :], uc[:, 0, :], uc[:, 1, :], ALU.mult).then_inc(S["u_ready"], 1)
            dve.wait_ge(S["u_ready"], 1)
            dve.wait_ge(S["omega_exp"], 3)
            rt(v.scalar_tensor_tensor(omE[:, 2, :], omE[:, 0, :], 0.0, omE[:, 1, :], op0=ALU.max, op1=ALU.add))
            rt(v.tensor_tensor(omE[:, 0, :], omE[:, 2, :], slopes, ALU.mult))
            for g in range(4):
                dve.wait_ge(S["xh_ready"], g + 1)
                v.tensor_tensor(xl[:, g * CH:(g + 1) * CH], xf[:, g * CH:(g + 1) * CH],
                                xh[:, g * CH:(g + 1) * CH].bitcast(f32), ALU.subtract).then_inc(S["xl_ready"], 1)
            for b in range(2):
                for a in range(2):
                    v.tensor_copy(QM[b][AUG:MROW, a, :], AQ[AUG:MROW, :]).then_inc(S["rows_ready"], 1)
                    v.tensor_copy(KM[b][MROW:MROW + 1, a, :], AQ[MROW:MROW + 1, :]).then_inc(S["rows_ready"], 1)
            dve.wait_ge(S["logit_psum"], 1)
            lg = SM[:, 0, :].rearrange("p (t e) -> p t e", e=E)
            rt(v.tensor_reduce(rsum[:, 0, :], lg, axis=AX.X, op=ALU.max))
            v.tensor_tensor(chosen, lg, rsum[:, 0, :].unsqueeze(2).to_broadcast([P, NT, E]), ALU.subtract
                            ).then_inc(S["rt_exp"], 1)
            dve.wait_ge(S["rt_exp"], 2)
            for t in range(NT):
                v.max(tops[:, t, :], prob[:, t, :]).then_inc(S["logit_done"], 1)
            dve.wait_ge(S["logit_done"], NT)
            for t in range(NT):
                v.match_replace(repl[:, t, :], tops[:, t, :], prob[:, t, :], -1.0).then_inc(S["logit_done"], 1)
            dve.wait_ge(S["logit_done"], 2 * NT)
            rt(v.tensor_scalar(chosen, repl, 0.0, None, ALU.is_lt))
            for g in range(4):
                last = v.tensor_copy(selr[:, :, g, :], chosen)
            last.then_inc(S["selr_ready"], 1)
            rt(v.tensor_tensor(repl, prob, chosen, ALU.mult))
            rt(v.tensor_reduce(rsum[:, 1, :], repl, axis=AX.X, op=ALU.add))
            rt(v.reciprocal(rsum[:, 2, :], rsum[:, 1, :]))
            v.tensor_tensor(XW[:, :, C:ROW], repl, rsum[:, 2, :].unsqueeze(2).to_broadcast([P, NT, E]), ALU.mult
                            ).then_inc(S["wts_ready"], 1)
            v.tensor_copy(CUM[:, N:N + CAP], slot_no)
            rt(v.memset(ONES, 1.0))
            for g in range(4):
                dve.wait_ge(S["selT_psum"], g + 1)
                v.tensor_tensor_scan(CUM[:, g * CH:(g + 1) * CH], ONES, ST[:, g % 2, :],
                                     0.0 if g == 0 else CUM[:, g * CH - 1:g * CH],
                                     ALU.mult, ALU.add).then_inc(S["selT_done"], 1)
                dve.wait_ge(S["selT_done"], g + 1)
            for h in range(4):
                last = v.max_index(idx[:, 8 * h:8 * h + 8], own_slot_no[:, 8 * h:8 * h + 8], CUM)
            rt(last)
            v.transpose(idxT[:, :], idx[:, :]).then_inc(S["idx_ready"], 1)
            dve.wait_ge(S["idx_ready"], 1)
            dve.wait_ge(S["table_out"], 32)
            rt(v.memset(ACC[:, :], 0.0))

            split_weights(0)
            for step in range(NC):
                prep("PRO", 0, 0, 0, step)
            for step in range(NC):
                prep_values("PRO", 0, 0, 0, step)
            for i in range(NC):
                max_chunk(0, i)

            def slot(s, b, a, kind, nxt):
                n = 2 * s + a
                first = FIRST_MAX[a]
                for i in range(NC):
                    if i >= 1:
                        split_probs(n, i - 1)
                    elif not (kind == "FIRST" and a == 0):
                        split_probs(n - 1, NC - 1)
                    if nxt and first <= i < first + 6:
                        max_chunk(n + 1, 2 * (i - first))
                        max_chunk(n + 1, 2 * (i - first) + 1)
                    if i == SUMS[1] + 1 and not (kind == "FIRST" and a == 0):
                        normalise(n - 1, 1 - a, s - 1 if a == 0 else s, 1)
                    if a == 0 and i == 8 and kind != "FIRST":
                        add_projection(kind, s, s - 1)
                    if a == 0 and kind != "LAST":
                        prep(kind, s, s + 1, 1 - b, i)
                    if a == 1:
                        moe_step(kind, s, b, i)
                        if kind != "LAST":
                            prep_values(kind, s, s + 1, 1 - b, i)
                    if i == SUMS[0] + 1:
                        normalise(n, a, s, 0)

            def period(s, b, kind):
                slot(s, b, 0, kind, True)
                slot(s, b, 1, kind, kind != "LAST")

            period(0, 0, "FIRST")
            with dve.Fori(0, (NPAIR - 2) // 2) as it:
                period(2 * it + 1, 1, "MID")
                period(2 * it + 2, 0, "MID")
            period(NPAIR - 1, 1, "LAST")
            split_probs(2 * NPAIR - 1, NC - 1)
            normalise(2 * NPAIR - 1, 1, NPAIR - 1, 1)
            add_projection("FIN", 0, NPAIR - 1)
            dve.wait_ge(S["res_in"], 16)
            for g in range(4):
                o, free = taken("FIN", 0, f"ft{g}")
                v.tensor_tensor(fin[:, 4 * g:4 * g + 4, :], o.rearrange("p (t c) -> p t c", c=C),
                                res[:, 4 * g:4 * g + 4, :], ALU.add).then_inc(S["final_ready"], 1)
                dve.wait_ge(S["final_ready"], g + 1)
                dve.sem_inc(free, 1)

        @block.gpsimd
        def _(pool):
            g_ = nc.gpsimd

            def stand(value):
                if not isinstance(value, int):
                    pool.sem_inc(S["pool_steps"], 1)
            g_.memset(ZR[:, :], 0.0).then_inc(S["zero_ready"], 1)
            g_.memset(eps[:, :], 1e-5).then_inc(S["pool_c"], 2)
            for b in range(2):
                g_.memset(VH[b][:, :, :, D:2 * D].bitcast(f32), 1.0)
                last = g_.memset(VL[b][:, :, :, D:2 * D].bitcast(f32), 0.0)
            last.then_inc(S["v_ones"], 1)

            def split(p):
                for t, done in ((0, S["lo_q_ready"]), (1, S["lo_k_ready"])):
                    pool.wait_ge(S["hi_ready"], 2 * p + t + 1)
                    stand(p)
                    g_.tensor_tensor(LO[:, t, :], RAW[:, t, :], HI[:, t, :].bitcast(f32), ALU.subtract
                                     ).then_inc(done, 1)

            def gather(s, b):
                if not isinstance(s, int) or s >= 2:
                    pool.wait_ge(S["yw_ready"], s - 1)
                    stand(s)
                g_.tensor_copy(idxc[b][:, :], idxT[:, bass.ds(2 * s, 2)]).then_inc(S["idxc_ready"], 1)
                pool.wait_ge(S["idxc_ready"], s + 1)
                stand(s)
                for e in range(2):
                    g_.indirect_dma_start(out=G[b][:, e, :], out_offset=None, in_=table,
                                          in_offset=bass.IndirectOffsetOnAxis(ap=idxc[b][:, e:e + 1], axis=0)
                                          ).then_inc(S["gather_in"], 16)
                pool.wait_ge(S["gather_in"], 32 * (s + 1))
                stand(s)

            def scatter(s, b):
                pool.wait_ge(S["yw_ready"], s + 1)
                stand(s)
                for e in range(2):
                    g_.indirect_dma_start(out=total,
                                          out_offset=bass.IndirectOffsetOnAxis(ap=idxc[b][:, e:e + 1], axis=0),
                                          in_=YW[:, e, :], in_offset=None, compute_op=ALU.add
                                          ).then_inc(S["scatter_done"], 16)
                    pool.wait_ge(S["scatter_done"], 32 * s + 16 * (e + 1))
                    stand(s)

            pool.wait_ge(S["idx_ready"], 1)
            pool.wait_ge(S["table_out"], 32)
            pool.wait_ge(S["total_out"], 32)
            gather(0, 0)
            split(0)

            def period(s, b, kind):
                if kind != "LAST":
                    split(s + 1)
                scatter(s, b)
                if kind != "LAST":
                    gather(s + 1, 1 - b)

            period(0, 0, "FIRST")
            with pool.Fori(0, (NPAIR - 2) // 2) as it:
                period(2 * it + 1, 1, "MID")
                period(2 * it + 2, 0, "MID")
            period(NPAIR - 1, 1, "LAST")


_INPUTS = ("x", "w3", "wproj", "qw", "kw", "om", "u", "gwt", "gup", "dwn", "cst", "augq")


def _constants(np):
    p, q = np.arange(P)[:, None], np.arange(P)[None, :]
    k = np.zeros((P, K_ALL), np.float32)
    k[:, K_ID:K_ID + P] = p == q
    k[:, K_MR:K_MR + P] = np.where(q > p, NEG, 0.0)
    k[:, K_MT:K_MT + P] = np.where(p > q, NEG, 0.0)
    k[:, K_NP] = -np.arange(P)
    k[:, K_SLOT:K_SLOT + P] = q + 1
    k[:, K_ONES:K_ONES + P] = (p // D == q // D) / D
    k[:, K_UM:K_UM + 2] = p // D == np.arange(2)[None, :]
    k[:, K_SL:K_SL + 2 * NPAIR] = -np.tile(2.0 ** (-8.0 * (np.arange(H) + 1) / H), B)[None, :]
    k[:, K_OWN:K_OWN + CAP // 4] = 32 * (p // 32) + np.arange(1, CAP // 4 + 1)[None, :]
    a = np.zeros((P, T), np.float32)
    i = np.arange(T)
    for t in range(TB):
        a[AUG + t] = a[AUG + TB + t] = i - P * t
    a[AUG + 2 * TB:AUG + 2 * TB + 2] = 1.0
    a[MROW] = 1.0
    return k, a


def kernel(L0_attn_x, L0_attn_Wq, L0_attn_Wk, L0_attn_Wv, L0_attn_Wproj, L0_attn_q_rms_w, L0_attn_k_rms_w,
           L0_attn_omega, L0_attn_u, L0_ffn_gate_weight, L0_ffn_gate_up_proj, L0_ffn_down_proj):
    import numpy as np
    import concourse.bacc as bacc
    from concourse.bass_utils import run_bass_kernel_spmd

    def pairs(w):
        return np.asarray(w).reshape(C, H // 2, 2 * D).transpose(1, 0, 2)

    cst, augq = _constants(np)
    arrays = {
        "x": np.asarray(L0_attn_x).reshape(N, C),
        "w3": np.concatenate([pairs(L0_attn_Wq), pairs(L0_attn_Wk), pairs(L0_attn_Wv)], axis=2),
        "wproj": np.asarray(L0_attn_Wproj).reshape(H // 2, 2 * D, C),
        "qw": np.tile(np.asarray(L0_attn_q_rms_w), 2)[:, None],
        "kw": np.tile(np.asarray(L0_attn_k_rms_w), 2)[:, None],
        "om": np.broadcast_to(np.tile(np.asarray(L0_attn_omega), B)[None, :], (P, 2 * NPAIR)),
        "u": np.tile(np.asarray(L0_attn_u).reshape(H // 2, 2 * D).T, (1, B)),
        "gwt": np.asarray(L0_ffn_gate_weight).T,
        "gup": np.asarray(L0_ffn_gate_up_proj).reshape(NPAIR, 2, 2 * F, C).transpose(0, 3, 1, 2).reshape(
            NPAIR, C, 4 * F),
        "dwn": np.asarray(L0_ffn_down_proj).reshape(NPAIR, 2, C, F).transpose(0, 3, 1, 2).reshape(NPAIR, F, 2 * C),
        "cst": cst,
        "augq": augq,
    }
    arrays = {k: np.ascontiguousarray(a) for k, a in arrays.items()}
    nc = bacc.Bacc("TRN2", target_bir_lowering=False, num_devices=1)
    ins = [nc.dram_tensor(f"in_{k}", arrays[k].shape, mybir.dt.from_np(arrays[k].dtype), kind="ExternalInput").ap()
           for k in _INPUTS]
    out = nc.dram_tensor("out", (N, C), mybir.dt.float32, kind="ExternalOutput").ap()
    layer(nc, *ins, out)
    r = run_bass_kernel_spmd(nc, [{f"in_{k}": a for k, a in arrays.items()}], core_ids=[0])
    return r.results[0]["out"].reshape(B, T, C)
```

```python
import concourse.bass as bass
from concourse import mybir
from contextlib import ExitStack

B, T, C = 2, 1024, 128
H, D = 16, 64
E, TOPK, CAP, F = 32, 8, 128, 96
P = 128
N = B * T
NT = N // P
TB = T // P
NPAIR = B * H // 2
ROW = C + E
NROWS = N + CAP
CH = 512
AUG = 64
MROW = 96
NEG = -1.0e30

K_ID, K_NP, K_SLOT, K_ONES, K_UM, K_SL, K_OWN = 0, 128, 129, 257, 385, 387, 419
K_END = K_OWN + CAP // 4
K_MR, K_MT, K_ALL = K_END, K_END + P, K_END + 2 * P

MAXC = []
for _ib in range(TB):
    _w = P * (_ib + 1)
    if _w > CH:
        MAXC += [(_ib, 0, CH, False), (_ib, CH, _w - CH, True)]
    else:
        MAXC += [(_ib, 0, _w, True)]
STC = []
for _c in range(2):
    for _jb in range(TB):
        _q0 = max(P * _jb, CH * _c)
        if _q0 < CH * (_c + 1):
            STC += [(_jb, _c, _q0, CH * (_c + 1) - _q0, _q0 == P * _jb)]
NC = len(STC)
HALF_DONE = max(i for i, _s in enumerate(STC) if _s[1] == 0)
LAG = 3
FIRST_MAX = (1, 3)
MAX_ROW = (9, 9)
SUMS = (10, 3)
VALUES = (9, 10)
PROJECT = (9, 10)
HI_ON_ACT = (0, 1, 2, 4, 5, 6, 7, 8, 10)
assert NC == len(MAXC) == 12

PREP = ["q0", "q1", "k0", "k1", "nq0", "nq1", "nk0", "nk1"]
USES = {
    "PRO": PREP + ["gate", "aug0", "aug1", "mb", "v0", "v1"],
    "FIRST": PREP + ["ma", "gate", "aug0", "aug1", "mx", "mgu", "meo", "mb", "v0", "v1"],
    "MID": PREP + ["ma", "pr0", "pr1", "gate", "aug0", "aug1", "mx", "mgu", "meo", "mb", "v0", "v1"],
    "LAST": ["ma", "pr0", "pr1", "mx", "mgu", "meo"],
    "FIN": ["pr0", "pr1"] + [f"ft{i}" for i in range(4)],
}
N_PRO, N_FIRST, N_MID, N_LAST = (len(USES[k]) for k in ("PRO", "FIRST", "MID", "LAST"))
assert N_PRO % 2 == 0 and N_FIRST % 2 == 0 and N_MID % 2 == 0 and N_LAST % 2 == 0


def use(kind, s, name):
    k = USES[kind].index(name)
    if kind == "PRO":
        base, half = 0, 0
    elif kind == "FIRST":
        base, half = N_PRO, N_PRO // 2
    elif kind == "MID":
        base = (s - 1) * N_MID + (N_PRO + N_FIRST)
        half = (s - 1) * (N_MID // 2) + (N_PRO + N_FIRST) // 2
    else:
        base = N_PRO + N_FIRST + (NPAIR - 2) * N_MID
        if kind == "FIN":
            base += N_LAST
        half = base // 2
    return k % 2, base + k + 1, half + k // 2


def wait(eng, sem, value):
    if isinstance(value, int) and value <= 0:
        return
    eng.wait_ge(sem, value)


def layer(nc, x, w3, wproj, qw, kw, om, u, gwt, gup, dwn, cst, augq, out):
    f32, r32, bf16, u32 = mybir.dt.float32, mybir.dt.float32r, mybir.dt.bfloat16, mybir.dt.uint32
    ALU, ACT, AX = mybir.AluOpType, mybir.ActivationFunctionType, mybir.AxisListType
    ctx = ExitStack()
    with ctx:
        def sb(name, shape, dt=f32):
            return ctx.enter_context(nc.sbuf_tensor(name, shape, dt))

        def sem(name):
            return ctx.enter_context(nc.semaphore(name))

        table = nc.dram_tensor("token_table", [NROWS, ROW], f32).ap()
        total = nc.dram_tensor("residual_and_experts", [NROWS, C], f32).ap()

        K = sb("consts", [P, K_END])
        ident = K[:, K_ID:K_ID + P]
        neg_p = K[:, K_NP:K_NP + 1]
        slot_no = K[:, K_SLOT:K_SLOT + P]
        blk_ones = K[:, K_ONES:K_ONES + P]
        head_of = K[:, K_UM:K_UM + 2]
        slopes = K[:, K_SL:K_SL + 2 * NPAIR]
        own_slot_no = K[:, K_OWN:K_OWN + CAP // 4]
        maskb = sb("mask_bf16", [P, 3 * P], bf16)
        ident_b, mask_qk, mask_kq = maskb[:, 0:P], maskb[:, P:2 * P], maskb[:, 2 * P:3 * P]
        qwk = sb("qk_norm_weights", [P, 3])
        omE = sb("minus_omega", [P, 3, 2 * NPAIR])
        uc = sb("u_columns", [P, 3, NPAIR])
        U2 = sb("u_pair", [P, 2])
        eps = sb("eps", [P, 2])
        gw = sb("router_weight", [P, E])

        PRT = sb("probs", [P, 4 * CH + CAP])
        PR = PRT[:, 0:4 * CH].rearrange("p (i w) -> p i w", w=CH)
        X = PRT[:, 0:N].rearrange("p (t c) -> p t c", c=C)
        ACC = sb("attn_out_T", [P, 4 * T])
        acc = ACC[:, 0:N]
        R = ACC[:, 3 * T:4 * T].rearrange("p (j r) -> p j r", r=P)
        xh, xl = sb("xn_hi", [P, N], r32), sb("xn_lo", [P, N], r32)

        wraw = sb("w_raw", [P, 3 * P])
        wh, wl = sb("w_hi", [P, 3 * P], r32), sb("w_lo", [P, 3 * P], r32)
        RAW = sb("qk", [P, 2, T])
        SQ = sb("qk_sq", [P, 2, T])
        LO = SQ
        HIT = sb("qk_hi", [P, N], r32)
        HI = HIT[:, :].rearrange("p (a t) -> p a t", a=2)
        GT = sb("gate_work", [P, 6, 2 * TB])
        QM, KM = ([sb(f"{n}{i}", [P, 2, T], r32) for i in range(2)] for n in ("QM", "KM"))
        XX = [sb(f"cross{i}", [P, 2, 2, T], r32) for i in range(2)]
        QX, KX = ([XX[i][:, k, :, :] for i in range(2)] for k in range(2))
        VH, VL = ([sb(f"{n}{i}", [P, TB, 2, P], r32) for i in range(2)] for n in ("v_hi", "v_lo"))

        mx = sb("row_max_halves", [P, 4, 2])
        mcol = sb("row_max", [P, TB])
        mrow = sb("minus_max_row", [TB, 2, P], r32)
        PHL = sb("probs_parts", [P, 2, 4, CH], r32)
        PH, PL = PHL[:, 0, :, :], PHL[:, 1, :, :]
        RLT = sb("inverse_sums", [P, T], r32)
        RL = RLT[0:D, :].bitcast(f32)
        Y = sb("y", [P, T])
        wp = sb("w_proj", [P, C])

        idxT = sb("slot_token", [P, E], u32)
        idxc = [sb(f"slot_token_pair{i}", [P, 2], u32) for i in range(2)]
        G = [sb(f"gathered{i}", [P, 2, ROW]) for i in range(2)]
        wgu = [sb(f"w_gate_up{i}", [P, 2, 2 * F]) for i in range(2)]
        wdn = [sb(f"w_down{i}", [F, 2, C]) for i in range(2)]
        XG = sb("gathered_T", [P, 2 * CAP])
        SGP = sb("silu_work", [P, 3, 2 * CAP])
        SG = SGP[0:F, :, :]
        YW = sb("expert_rows", [P, 2, C])

        xf = HIT[:, :].bitcast(f32)

        def inside(host, *sizes):
            at = [sum(sizes[:i]) for i in range(len(sizes) + 1)]
            return [host[:, at[i]:at[i + 1]] for i in range(len(sizes))]

        XW, ONES = inside(ACC, NT * ROW, CH)
        XW = XW.rearrange("p (t r) -> p t r", r=ROW)
        prob, repl, chosen = (m.rearrange("p (t e) -> p t e", e=E)
                              for m in inside(HIT[:, :].bitcast(f32), NT * E, NT * E, NT * E))
        CUM = PRT[:, :]
        masks, ZR = inside(Y, 2 * P, ROW)
        selr = Y[:, :].bitcast(bf16).rearrange("p (t g e) -> p t g e", g=4, e=E)
        rows, rows_f = RLT[0:MROW - AUG + 1, :], RLT[D:D + MROW - AUG + 1, :].bitcast(f32)
        stats = SGP[:, 0, 0:6 * NT].rearrange("p (t k) -> p t k", k=6)
        mv = SGP[:, 0, 6 * NT:8 * NT].rearrange("p (t k) -> p t k", k=2)
        rs = SGP[:, 0, 8 * NT:10 * NT].rearrange("p (k t) -> p k t", k=2)
        tops = SGP[:, 1, 0:NT * TOPK].rearrange("p (t k) -> p t k", k=TOPK)
        rsum = SGP[:, 2, 0:3 * NT].rearrange("p (k t) -> p k t", k=3)
        idx = SGP[:, 2, 3 * NT:3 * NT + E].bitcast(u32)
        res = RAW[:, :, :].rearrange("p a (t c) -> p (a t) c", c=C)
        fin = SQ[:, :, :].rearrange("p a (t c) -> p (a t) c", c=C)

        SM = ctx.enter_context(nc.psum_tensor("SM", [P, 2, CH], f32))
        ST = ctx.enter_context(nc.psum_tensor("ST", [P, 2, CH], f32))
        AV = ctx.enter_context(nc.psum_tensor("AV", [P, T], f32))
        XB = ctx.enter_context(nc.psum_tensor("XB", [P, 2, CH], f32))

        S = {n: sem(n) for n in (
            "const_in", "x_in", "w_in", "wp_in", "we_in", "gather_in", "table_out", "total_out", "out_out",
            "consts_ready", "mask_ready", "stats_ready", "ln_var", "ln_rstd", "xn_ready", "zero_ready",
            "xt_psum", "xt_copied", "xh_ready", "xl_ready", "logit_psum", "logit_done", "selr_ready",
            "selT_psum", "selT_done", "idx_ready", "rt", "rt_exp", "omega_exp", "u_sq",
            "u_psum", "u_ln", "u_ready", "rows_ready", "rows_in", "v_ones", "bias_zero", "acc_zero", "wts_ready",
            "eps_ready", "pool_steps", "sp_steps",
            "spare_ready", "spare_free0", "spare_free1",
            "w_hi_ready", "w_lo_ready", "raw_ready", "sq_ready", "rs_ready", "qk_ready", "hi_ready",
            "lo_q_ready", "lo_k_ready", "main_in", "cross_in", "v_hi_ready", "v_ready", "u2_ready", "gl_ready",
            "gate_abs", "gate_exp", "gate_ln", "gs", "bias_ready", "bias_rows_0", "bias_rows_1",
            "max_scores", "max_taken", "max_ready", "mrow_ready", "mrow_in", "scores", "probs_ready",
            "hi_act", "hi_dve", "lo_probs", "pv_done", "sum_ln", "sum_inv", "y_ready", "proj_added",
            "idxc_ready", "xg_ready", "sg_exp", "sg", "h_ready", "yw_ready", "scatter_done", "final_ready", "res_in")}
        spare_free = [S["spare_free0"], S["spare_free1"]]
        block = ctx.enter_context(nc.Block())

        MAIN, CROSS = 4, 8

        def hi_ready(n, i):
            mine = [k for k in range(NC) if (k in HI_ON_ACT) == (i in HI_ON_ACT)]
            return S["hi_act" if i in HI_ON_ACT else "hi_dve"], len(mine) * n + (mine.index(i) + 1)

        def batch(s):
            return s // (H // 2)

        def pair(s):
            return s % (H // 2)

        @block.sync
        def _(sp):
            sp.dma_start(X[:, :, :], x.rearrange("(t p) c -> p t c", p=P)).then_inc(S["x_in"], 16)
            for dst, src in ((K[:, :], cst[:, 0:K_END]), (masks, cst[:, K_END:K_ALL]), (rows_f, augq),
                             (qwk[:, 0:1], qw), (qwk[:, 1:2], kw),
                             (omE[:, 0, :], om), (uc[:, 0, :], u), (gw[:, :], gwt)):
                sp.dma_start(dst, src).then_inc(S["const_in"], 16)

            def stand(value):
                if not isinstance(value, int):
                    sp.sem_inc(S["sp_steps"], 1)

            def load_w(s, wait_for):
                if wait_for is not None:
                    wait(sp, S["w_hi_ready"], wait_for)
                    wait(sp, S["w_lo_ready"], wait_for)
                sp.dma_start(wraw[:, :], w3[bass.ds(pair(s), 1), :, :].rearrange("a p n -> (a p) n")
                             ).then_inc(S["w_in"], 16)

            def spread(s, b):
                wait(sp, S["pv_done"], NC * (2 * s - 2))
                stand(s)
                for t in (0, 1):
                    sp.wait_ge(S["hi_ready"], 2 * s + t + 1)
                    main, cross = ((QM, QX), (KM, KX))[t]
                    for a in range(2):
                        src = HI[D * a:D * a + D, t, :].bitcast(f32)
                        sp.dma_start(main[b][0:D, a, :].bitcast(f32), src).then_inc(S["main_in"], 16)
                        sp.dma_start(cross[b][D * (1 - t):D * (2 - t), a, :].bitcast(f32), src
                                     ).then_inc(S["cross_in"], 16)
                for t in (0, 1):
                    sp.wait_ge(S[("lo_q_ready", "lo_k_ready")[t]], s + 1)
                    cross = (QX, KX)[t]
                    for a in range(2):
                        sp.dma_start(cross[b][D * t:D * t + D, a, :].bitcast(f32), LO[D * a:D * a + D, t, :]
                                     ).then_inc(S["cross_in"], 16)

            def load_experts(s, b):
                if not isinstance(s, int) or s >= 2:
                    sp.wait_ge(S["yw_ready"], s - 1)
                sp.dma_start(wgu[b][:, :, :], gup[bass.ds(s, 1), :, :].rearrange("a p (e n) -> (a p) e n", e=2)
                             ).then_inc(S["we_in"], 16)
                sp.dma_start(wdn[b][:, :, :], dwn[bass.ds(s, 1), :, :].rearrange("a p (e n) -> (a p) e n", e=2)
                             ).then_inc(S["we_in"], 16)

            load_w(0, None)
            sp.wait_ge(S["zero_ready"], 1)
            sp.dma_start(table[N:NROWS, :], ZR[:, :]).then_inc(S["table_out"], 16)
            sp.dma_start(total[N:NROWS, :], ZR[:, 0:C]).then_inc(S["total_out"], 16)
            sp.wait_ge(S["x_in"], 16)
            sp.dma_start(total[0:N, :].rearrange("(t p) c -> p t c", p=P), X[:, :, :]).then_inc(S["total_out"], 16)
            load_w(1, 1)
            sp.wait_ge(S["rows_ready"], 1)
            for b in range(2):
                for a in range(2):
                    sp.dma_start(QM[b][AUG:MROW, a, :].bitcast(f32), rows[0:MROW - AUG, :].bitcast(f32)
                                 ).then_inc(S["rows_in"], 16)
                    sp.dma_start(KM[b][MROW:MROW + 1, a, :].bitcast(f32),
                                 rows[MROW - AUG:MROW - AUG + 1, :].bitcast(f32)).then_inc(S["rows_in"], 16)
            sp.wait_ge(S["wts_ready"], 1)
            sp.dma_start(table[0:N, :].rearrange("(t p) c -> p t c", p=P), XW[:, :, :]).then_inc(S["table_out"], 16)
            spread(0, 0)

            def period(s, b, kind):
                if kind != "LAST":
                    load_w(s + 2, s + 2)
                load_experts(s, b)
                if kind != "LAST":
                    spread(s + 1, 1 - b)
                if kind != "FIRST":
                    _, ready, _ = use(kind, s, "pr1")
                    sp.wait_ge(S["spare_ready"], ready)
                sp.dma_start(wp[:, :], wproj[bass.ds(pair(s), 1), :, :].rearrange("a p n -> (a p) n")
                             ).then_inc(S["wp_in"], 16)

            period(0, 0, "FIRST")
            with sp.Fori(0, (NPAIR - 2) // 2) as it:
                period(2 * it + 1, 1, "MID")
                period(2 * it + 2, 0, "MID")
            period(NPAIR - 1, 1, "LAST")
            sp.wait_ge(S["scatter_done"], 32 * NPAIR)
            sp.dma_start(res, total[0:N, :].rearrange("(t p) c -> p t c", p=P)).then_inc(S["res_in"], 16)
            for g in range(4):
                sp.wait_ge(S["final_ready"], g + 1)
                sp.dma_start(out[g * CH:(g + 1) * CH, :].rearrange("(t p) c -> p t c", p=P),
                             fin[:, 4 * g:4 * g + 4, :]).then_inc(S["out_out"], 16)
            sp.wait_ge(S["out_out"], 64)
            sp.wait_ge(S["table_out"], 32)
            sp.wait_ge(S["total_out"], 32)

        @block.tensor
        def _(pe):
            mm = nc.tensor.matmul

            def mm3(o, whi, wlo, xhi, xlo):
                mm(o, wlo, xhi, start=True, stop=False)
                mm(o, whi, xlo, start=False, stop=False)
                return mm(o, whi, xhi, start=False, stop=True)

            def spare(kind, s, name):
                bank, ready, earlier = use(kind, s, name)
                wait(pe, spare_free[bank], earlier)
                return XB[:, bank, :]

            def project(kind, s, name, bt):
                o = spare(kind, s, name)
                i, c = "qk".index(name[0]), int(name[1])
                w, tokens = slice(i * P, (i + 1) * P), slice(bt * T + c * CH, bt * T + (c + 1) * CH)
                mm3(o, wh[:, w], wl[:, w], xh[:, tokens], xl[:, tokens]).then_inc(S["spare_ready"], 1)

            def values(kind, s, name, bt):
                o = spare(kind, s, name)
                for j in range(4):
                    block = slice(bt * T + int(name[1]) * CH + j * P, bt * T + int(name[1]) * CH + (j + 1) * P)
                    last = mm3(o[:, j * P:(j + 1) * P], xh[:, block], xl[:, block], wh[:, 2 * P:], wl[:, 2 * P:])
                last.then_inc(S["spare_ready"], 1)

            def head_norm(kind, s, name):
                o = spare(kind, s, name)
                t, c = "qk".index(name[1]), int(name[2])
                mm(o, blk_ones, SQ[:, t, c * CH:(c + 1) * CH], start=True, stop=True).then_inc(S["spare_ready"], 1)

            def gate(kind, s):
                o = spare(kind, s, "gate")
                for j in range(TB):
                    last = mm(o[:, 2 * j:2 * j + 2], RAW[:, 1, j * P:(j + 1) * P], U2[:, :], start=True, stop=True)
                last.then_inc(S["spare_ready"], 1)

            def bias_rows(kind, s, name):
                o = spare(kind, s, name)
                c = int(name[3])
                for j in range(4):
                    last = nc.tensor.transpose(o[:, j * P:(j + 1) * P], R[:, 4 * c + j, :], ident)
                last.then_inc(S["spare_ready"], 1)

            def prep(kind, s, p, bt, step):
                if step == 1:
                    pe.wait_ge(S["w_hi_ready"], p + 1)
                    pe.wait_ge(S["w_lo_ready"], p + 1)
                    for n in ("q0", "q1"):
                        project(kind, s, n, bt)
                elif step == 3:
                    for n in ("k0", "k1"):
                        project(kind, s, n, bt)
                elif step == 5:
                    pe.wait_ge(S["sq_ready"], 2 * p + 1)
                    for n in ("nq0", "nq1"):
                        head_norm(kind, s, n)
                elif step == 7:
                    pe.wait_ge(S["sq_ready"], 2 * p + 2)
                    for n in ("nk0", "nk1"):
                        head_norm(kind, s, n)
                elif step == 10:
                    pe.wait_ge(S["qk_ready"], 2 * p + 2)
                    pe.wait_ge(S["u2_ready"], p + 1)
                    gate(kind, s)

            def prep_values(kind, s, p, bt, step):
                if step == 1:
                    pe.wait_ge(S["bias_ready"], p + 1)
                    for n in ("aug0", "aug1"):
                        bias_rows(kind, s, n)
                elif step in VALUES:
                    values(kind, s, f"v{VALUES.index(step)}", bt)

            def max_chunk(n, b, a, i):
                ib, j0, w, diag = MAXC[i]
                wait(pe, S["max_taken"], NC * n + i - 1)
                o = SM[:, i % 2, 0:w]
                last = mm(o, QM[b][0:MROW, a, ib * P:(ib + 1) * P], KM[b][0:MROW, a, j0:j0 + w],
                          start=True, stop=not diag)
                if diag:
                    last = mm(SM[:, i % 2, w - P:w], ident_b, mask_qk, start=False, stop=True)
                last.then_inc(S["max_scores"], 1)

            def max_row(kind, s, name, n):
                o = spare(kind, s, name)
                pe.wait_ge(S["max_ready"], n + 1)
                nc.tensor.transpose(o[0:TB, 0:P], mcol[:, :], ident).then_inc(S["spare_ready"], 1)

            def score_chunk(n, b, a, i):
                jb, c, q0, w, diag = STC[i]
                wait(pe, S["probs_ready"], NC * n + i - 1)
                o = ST[:, i % 2, 0:w]
                keys = slice(jb * P, (jb + 1) * P)
                mm(o, KX[b][:, a, keys], QX[b][:, a, q0:q0 + w], start=True, stop=False)
                last = mm(o, KM[b][0:MROW + 1, a, keys], QM[b][0:MROW + 1, a, q0:q0 + w], start=False, stop=not diag)
                if diag:
                    last = mm(ST[:, i % 2, 0:P], ident_b, mask_kq, start=False, stop=True)
                last.then_inc(S["scores"], 1)

            def moe_step(kind, s, b, step):
                if step == 2:
                    pe.wait_ge(S["gather_in"], 32 * (s + 1))
                    o = spare(kind, s, "mx")
                    for e in range(2):
                        last = nc.tensor.transpose(o[:, e * P:(e + 1) * P], G[b][:, e, 0:C], ident)
                    last.then_inc(S["spare_ready"], 1)
                elif step == 4:
                    pe.wait_ge(S["xg_ready"], s + 1)
                    pe.wait_ge(S["we_in"], 32 * (s + 1))
                    o = spare(kind, s, "mgu")
                    for gu in range(2):
                        for e in range(2):
                            at = gu * 2 * CAP + e * CAP
                            last = mm(o[0:F, at:at + CAP], wgu[b][:, e, gu * F:(gu + 1) * F],
                                      XG[:, e * CAP:(e + 1) * CAP], start=True, stop=True)
                    last.then_inc(S["spare_ready"], 1)
                elif step == 8:
                    pe.wait_ge(S["h_ready"], s + 1)
                    o = spare(kind, s, "meo")
                    for e in range(2):
                        last = mm(o[:, e * C:(e + 1) * C], SG[:, 2, e * CAP:(e + 1) * CAP], wdn[b][:, e, :],
                                  start=True, stop=True)
                    last.then_inc(S["spare_ready"], 1)

            def project_out(kind, s, p, halves):
                if 0 in halves:
                    pe.wait_ge(S["y_ready"], 4 * p + 4)
                    pe.wait_ge(S["wp_in"], 16 * (p + 1))
                for c in halves:
                    o = spare(kind, s, f"pr{c}")
                    mm(o, wp[:, :], Y[:, c * CH:(c + 1) * CH], start=True, stop=True).then_inc(S["spare_ready"], 1)

            pe.wait_ge(S["consts_ready"], 1)
            pe.wait_ge(S["u_sq"], 1)
            mm(AV[:, 0:NPAIR], blk_ones, uc[:, 1, :], start=True, stop=True).then_inc(S["u_psum"], 1)
            for g in range(4):
                pe.wait_ge(S["xn_ready"], g + 1)
                wait(pe, S["xt_copied"], g - 1)
                for j in range(4):
                    last = nc.tensor.transpose(ST[:, g % 2, j * P:(j + 1) * P], XW[:, 4 * g + j, 0:C], ident)
                last.then_inc(S["xt_psum"], 1)
            for t in range(NT):
                if t % 4 == 0:
                    pe.wait_ge(S["xt_copied"], t // 4 + 1)
                last = mm(SM[:, 0, t * E:(t + 1) * E], xf[:, t * P:(t + 1) * P], gw[:, :], start=True, stop=True)
            last.then_inc(S["logit_psum"], 1)
            pe.wait_ge(S["xh_ready"], 4)
            pe.wait_ge(S["xl_ready"], 4)
            pe.wait_ge(S["u_ready"], 1)
            for step in range(NC):
                prep("PRO", 0, 0, 0, step)
                if step == 7:
                    pe.wait_ge(S["selr_ready"], 1)
                    pe.wait_ge(S["mask_ready"], 1)
                    for g in range(4):
                        o = (ST, SM)[g // 2][:, g % 2, :]
                        for j in range(4):
                            last = mm(o[:, j * P:(j + 1) * P],
                                      selr[:, 4 * g + j, :, :].rearrange("p g e -> p (g e)"), ident_b,
                                      start=True, stop=True)
                        last.then_inc(S["selT_psum"], 1)
            for step in range(VALUES[0]):
                prep_values("PRO", 0, 0, 0, step)
            pe.wait_ge(S["selT_done"], 4)

            def first_use(p, with_rows):
                pe.wait_ge(S["main_in"], 16 * MAIN * (p + 1))
                pe.wait_ge(S["bias_rows_0"], 2 * (p + 1))
                pe.wait_ge(S["bias_rows_1"], 2 * (p + 1))
                if with_rows:
                    pe.wait_ge(S["rows_in"], 16 * 8)

            first_use(0, True)
            for i in range(NC):
                max_chunk(0, 0, 0, i)
            max_row("PRO", 0, "mb", 0)
            for step in VALUES:
                prep_values("PRO", 0, 0, 0, step)

            def values_product(n, b, a, k):
                jb, c, q0, w, _ = STC[k]
                if k == 0 and a == 0:
                    pe.wait_ge(S["v_ready"], n + 2)
                if jb == 0:
                    wait(pe, S["y_ready"], 2 * n - 1 + c)
                o = AV[:, q0:q0 + w]
                hi_made, count = hi_ready(n, k)
                pe.wait_ge(hi_made, count)
                mm(o, VL[b][:, jb, a, :], PH[:, k % 4, 0:w], start=(jb == 0), stop=False)
                mm(o, VH[b][:, jb, a, :], PH[:, k % 4, 0:w], start=False, stop=False)
                pe.wait_ge(S["lo_probs"], NC * n + k + 1)
                mm(o, VH[b][:, jb, a, :], PL[:, k % 4, 0:w], start=False, stop=(jb == 4 * c + 3)
                   ).then_inc(S["pv_done"], 1)

            def slot(s, b, a, kind, bt, nxt):
                n = 2 * s + a
                nb = b if a == 0 else 1 - b
                pe.wait_ge(S["mrow_in"], 16 * (n + 1))
                if a == 0:
                    pe.wait_ge(S["cross_in"], 16 * CROSS * (s + 1))
                first = FIRST_MAX[a]
                for i in range(NC):
                    score_chunk(n, b, a, i)
                    if nxt and first <= i < first + 6:
                        if i == first and a == 1:
                            first_use(s + 1, False)
                        max_chunk(n + 1, nb, 1 - a, 2 * (i - first))
                    if i >= LAG:
                        values_product(n, b, a, i - LAG)
                    elif not (kind == "FIRST" and a == 0):
                        values_product(n - 1, 1 - b if a == 0 else b, 1 - a, NC + i - LAG)
                    if nxt and first <= i < first + 6:
                        max_chunk(n + 1, nb, 1 - a, 2 * (i - first) + 1)
                    if i == MAX_ROW[a] and nxt:
                        max_row(kind, s, "ma" if a == 0 else "mb", n + 1)
                    if a == 0 and i in PROJECT and kind != "FIRST":
                        project_out(kind, s, s - 1, (PROJECT.index(i),))
                    if a == 0 and kind != "LAST":
                        prep(kind, s, s + 1, bt, i)
                    if a == 1 and kind != "LAST":
                        prep_values(kind, s, s + 1, bt, i)
                    if a == 1:
                        moe_step(kind, s, b, i)

            def period(s, b, kind, bt):
                slot(s, b, 0, kind, bt, True)
                slot(s, b, 1, kind, bt, kind != "LAST")

            pe.wait_ge(S["v_ones"], 1)
            period(0, 0, "FIRST", 0)
            with pe.Fori(0, (NPAIR // 2 - 2) // 2) as it:
                period(2 * it + 1, 1, "MID", 0)
                period(2 * it + 2, 0, "MID", 0)
            with pe.Fori(0, NPAIR // 4) as it:
                period(2 * it + (NPAIR // 2 - 1), 1, "MID", 1)
                period(2 * it + NPAIR // 2, 0, "MID", 1)
            period(NPAIR - 1, 1, "LAST", 1)
            for k in range(NC - LAG, NC):
                values_product(2 * NPAIR - 1, 1, 1, k)
            project_out("FIN", 0, NPAIR - 1, (0, 1))
            pe.wait_ge(S["proj_added"], 2 * NPAIR)
            for g in range(4):
                o = spare("FIN", 0, f"ft{g}")
                for j in range(4):
                    t = 4 * g + j
                    last = nc.tensor.transpose(o[:, j * P:(j + 1) * P], acc[:, t * P:(t + 1) * P], ident)
                last.then_inc(S["spare_ready"], 1)

        @block.scalar
        def _(act):
            fn = nc.scalar.activation

            def taken(kind, s, name):
                bank, ready, _ = use(kind, s, name)
                act.wait_ge(S["spare_ready"], ready)
                return XB[:, bank, :], spare_free[bank]

            def split_weights(p):
                act.wait_ge(S["w_in"], 16 * (p + 1))
                fn(wh[:, :], wraw[:, :], ACT.Copy).then_inc(S["w_hi_ready"], 1)

            def prep(kind, s, p, pb, step):
                if step in (2, 4):
                    t = (step - 2) // 2
                    wait(act, S[("lo_q_ready", "lo_k_ready")[t]], p)
                    wait(act, S["cross_in"], 16 * CROSS * p)
                    for c in range(2):
                        o, free = taken(kind, s, f"{'qk'[t]}{c}")
                        half = slice(c * CH, (c + 1) * CH)
                        fn(RAW[:, t, half], o, ACT.Copy).then_inc(S["raw_ready"], 1)
                        act.wait_ge(S["raw_ready"], 4 * p + 2 * t + c + 1)
                        act.sem_inc(free, 1)
                    fn(SQ[:, t, :], RAW[:, t, :], ACT.Square).then_inc(S["sq_ready"], 1)
                elif step in (6, 8):
                    t = (step - 6) // 2
                    for c in range(2):
                        o, free = taken(kind, s, f"n{'qk'[t]}{c}")
                        fn(SQ[:, t, c * CH:(c + 1) * CH], o, ACT.Ln, bias=eps[:, 0:1]).then_inc(free, 1)
                        act.wait_ge(free, use(kind, s, f"n{'qk'[t]}{c}")[2] + 1)
                    fn(SQ[:, t, :], SQ[:, t, :], ACT.Exp, scale=-0.5).then_inc(S["rs_ready"], 1)
                elif step in (9, 10):
                    t = step - 9
                    act.wait_ge(S["qk_ready"], 2 * p + t + 1)
                    wait(act, S["main_in"], 16 * MAIN * p)
                    wait(act, S["cross_in"], 16 * CROSS * p)
                    fn(HI[:, t, :], RAW[:, t, :], ACT.Copy).then_inc(S["hi_ready"], 1)
                elif step == 11:
                    act.wait_ge(S["gl_ready"], p + 1)
                    fn(GT[:, 1, :], GT[:, 0, :], ACT.Abs).then_inc(S["gate_abs"], 1)
                    act.wait_ge(S["gate_abs"], p + 1)
                    fn(GT[:, 2, :], GT[:, 1, :], ACT.Exp, scale=-1.0).then_inc(S["gate_exp"], 1)
                    act.wait_ge(S["gate_exp"], p + 1)
                    fn(GT[:, 1, :], GT[:, 2, :], ACT.Ln, bias=1.0).then_inc(S["gate_ln"], 1)

            def prep_values(kind, s, p, pb, step):
                if step == 1:
                    wait(act, S["pv_done"], NC * (2 * p - 2))
                    o, free = taken(kind, s, "aug0")
                    for a in range(2):
                        fn(KM[pb][AUG:AUG + 32, a, 0:CH], o[AUG + 32 * a:AUG + 32 * a + 32, :],
                           ACT.Copy).then_inc(S["bias_rows_0"], 1)
                    act.wait_ge(S["bias_rows_0"], 2 * p + 2)
                    act.sem_inc(free, 1)
                elif step - 1 in VALUES:
                    c = VALUES.index(step - 1)
                    o, _ = taken(kind, s, f"v{c}")
                    fn(VH[pb][:, 4 * c:4 * c + 4, :, 0:D], o.rearrange("p (j a d) -> p j a d", j=4, a=2),
                       ACT.Copy).then_inc(S["v_hi_ready"], 1)
                    if c == 1:
                        split_weights(p + 1)

            def max_row(kind, s, name, n, b, a, par):
                o, free = taken(kind, s, name)
                wait(act, S["mrow_in"], 16 * (n - 1))
                fn(mrow[:, par, :], o[0:TB, 0:P], ACT.Copy, scale=-1.0).then_inc(S["mrow_ready"], 1)
                act.wait_ge(S["mrow_ready"], n + 1)
                act.sem_inc(free, 1)
                act.dma_start(QM[b][MROW:MROW + 1, a, :].rearrange("o (k q) -> o k q", q=P).bitcast(f32),
                              mrow[:, par, :].bitcast(f32)).then_inc(S["mrow_in"], 16)

            def inverse_sums(n, c):
                act.wait_ge(S["pv_done"], NC * n + (HALF_DONE + 1 if c == 0 else NC))
                wait(act, S["y_ready"], 2 * n - 1 + c)
                half = RL[:, c * CH:(c + 1) * CH]
                fn(half, AV[D:2 * D, c * CH:(c + 1) * CH], ACT.Ln).then_inc(S["sum_ln"], 1)
                act.wait_ge(S["sum_ln"], 2 * n + c + 1)
                fn(half, half, ACT.Exp, scale=-1.0).then_inc(S["sum_inv"], 1)

            def moe_step(kind, s, step):
                if step == 3:
                    o, free = taken(kind, s, "mx")
                    fn(XG[:, :], o[:, 0:2 * CAP], ACT.Copy).then_inc(S["xg_ready"], 1)
                    act.wait_ge(S["xg_ready"], s + 1)
                    act.sem_inc(free, 1)
                elif step == 5:
                    bank, ready, _ = use(kind, s, "mgu")
                    act.wait_ge(S["spare_ready"], ready)
                    fn(SG[:, 0, :], XB[0:F, bank, 0:2 * CAP], ACT.Exp, scale=-1.0).then_inc(S["sg_exp"], 1)
                    act.wait_ge(S["sg_exp"], 3 * s + 1)
                    fn(SG[:, 1, :], SG[:, 0, :], ACT.Ln, bias=1.0).then_inc(S["sg_exp"], 1)
                    act.wait_ge(S["sg_exp"], 3 * s + 2)
                    fn(SG[:, 0, :], SG[:, 1, :], ACT.Exp, scale=-1.0).then_inc(S["sg_exp"], 1)

            act.preload_act_table_set("natural_log_exp_and_others")
            act.wait_ge(S["const_in"], 16 * 8)
            act.wait_ge(S["eps_ready"], 2)
            fn(omE[:, 1, :], omE[:, 0, :], ACT.Abs).then_inc(S["omega_exp"], 1)
            act.wait_ge(S["omega_exp"], 1)
            fn(omE[:, 2, :], omE[:, 1, :], ACT.Exp, scale=-1.0).then_inc(S["omega_exp"], 1)
            act.wait_ge(S["omega_exp"], 2)
            fn(omE[:, 1, :], omE[:, 2, :], ACT.Ln, bias=1.0).then_inc(S["omega_exp"], 1)
            act.wait_ge(S["ln_var"], NT)
            fn(rs[:, 0, :], mv[:, :, 1], ACT.Ln, bias=eps[:, 0:1]).then_inc(S["ln_rstd"], 1)
            act.wait_ge(S["ln_rstd"], 1)
            fn(rs[:, 1, :], rs[:, 0, :], ACT.Exp, scale=-0.5).then_inc(S["ln_rstd"], 1)
            act.wait_ge(S["u_ln"], 1)
            fn(uc[:, 2, :], uc[:, 1, :], ACT.Ln).then_inc(S["u_ln"], 1)
            act.wait_ge(S["u_ln"], 2)
            fn(uc[:, 1, :], uc[:, 2, :], ACT.Exp, scale=-0.5).then_inc(S["u_ln"], 1)
            split_weights(0)
            for g in range(4):
                act.wait_ge(S["xt_copied"], g + 1)
                fn(xh[:, g * CH:(g + 1) * CH], xf[:, g * CH:(g + 1) * CH], ACT.Copy).then_inc(S["xh_ready"], 1)
            for step in range(NC):
                if step == 9:
                    act.wait_ge(S["wts_ready"], 1)
                prep("PRO", 0, 0, 0, step)
                if step == 2:
                    act.wait_ge(S["rt_exp"], 1)
                    fn(prob, chosen, ACT.Exp).then_inc(S["rt_exp"], 1)
            for step in range(VALUES[0]):
                prep_values("PRO", 0, 0, 0, step)
            max_row("PRO", 0, "mb", 0, 0, 0, 0)
            for step in VALUES:
                prep_values("PRO", 0, 0, 0, step + 1)
            act.wait_ge(S["total_out"], 32)
            act.wait_ge(S["idx_ready"], 1)
            act.wait_ge(S["rows_in"], 16 * 8)

            def slot(s, b, a, kind, nxt):
                n = 2 * s + a
                for i in range(NC):
                    jb, c, q0, w, _ = STC[i]
                    act.wait_ge(S["scores"], NC * n + i + 1)
                    wait(act, S["lo_probs"], NC * n + i - 3)
                    if i in HI_ON_ACT:
                        wait(act, S["pv_done"], NC * n + i - 3)
                        fn(PH[:, i % 4, 0:w], ST[:, i % 2, 0:w], ACT.Exp).then_inc(S["hi_act"], 1)
                    fn(PR[:, i % 4, 0:w], ST[:, i % 2, 0:w], ACT.Exp).then_inc(S["probs_ready"], 1)
                    if i == MAX_ROW[a] and nxt:
                        nb = b if a == 0 else 1 - b
                        max_row(kind, s, "ma" if a == 0 else "mb", n + 1, nb, 1 - a, 1 - a)
                    if i == SUMS[1] and not (kind == "FIRST" and a == 0):
                        inverse_sums(n - 1, 1)
                    if i == SUMS[0]:
                        inverse_sums(n, 0)
                    if a == 0 and kind != "LAST":
                        prep(kind, s, s + 1, 1 - b, i)
                    if a == 1:
                        moe_step(kind, s, i)
                        if kind != "LAST":
                            prep_values(kind, s, s + 1, 1 - b, i)

            def period(s, b, kind):
                slot(s, b, 0, kind, True)
                slot(s, b, 1, kind, kind != "LAST")

            period(0, 0, "FIRST")
            with act.Fori(0, (NPAIR - 2) // 2) as it:
                period(2 * it + 1, 1, "MID")
                period(2 * it + 2, 0, "MID")
            period(NPAIR - 1, 1, "LAST")
            inverse_sums(2 * NPAIR - 1, 1)

        @block.vector
        def _(dve):
            v = nc.vector

            def taken(kind, s, name):
                bank, ready, _ = use(kind, s, name)
                dve.wait_ge(S["spare_ready"], ready)
                return XB[:, bank, :], spare_free[bank]

            def diag(row0):
                return bass.AP(ACC[:, :].tensor, 3 * T + AUG + row0, [[4 * T, P], [P + 1, TB], [32, 2]])

            def gate_bias(p):
                def step(k):
                    return GS * p + k
                GS = 4
                dve.wait_ge(S["gate_ln"], p + 1)
                v.scalar_tensor_tensor(GT[:, 3, :], GT[:, 0, :], 0.0, GT[:, 1, :], op0=ALU.max, op1=ALU.add
                                       ).then_inc(S["gs"], 1)
                dve.wait_ge(S["gs"], step(1))
                v.tensor_tensor(GT[:, 4, :].rearrange("p (j a) -> p j a", a=2),
                                GT[:, 3, :].rearrange("p (j a) -> p j a", a=2),
                                omE[:, 0, bass.ds(2 * p, 2)].unsqueeze(1).to_broadcast([P, TB, 2]), ALU.mult
                                ).then_inc(S["gs"], 1)
                dve.wait_ge(S["gs"], step(2))
                g3 = GT[:, 4, :].rearrange("p (j a) -> p j a", a=2)
                j3 = GT[:, 5, :].rearrange("p (j a) -> p j a", a=2)
                v.tensor_scalar(GT[:, 5, :], GT[:, 4, :], neg_p, None, ALU.mult).then_inc(S["gs"], 1)
                v.tensor_copy(diag(0).bitcast(r32), g3)
                dve.wait_ge(S["gs"], step(3))
                Rv = R[:, :, AUG:AUG + 64].rearrange("p j (a r) -> p j a r", a=2)
                v.tensor_copy(Rv[:, :, :, 16].bitcast(r32), j3).then_inc(S["gs"], 1)
                dve.wait_ge(S["gs"], step(4))
                v.tensor_tensor(diag(8), g3, diag(0), ALU.subtract)
                v.tensor_tensor(Rv[:, :, :, 17], j3, Rv[:, :, :, 16], ALU.subtract).then_inc(S["bias_ready"], 1)

            def split_weights(p):
                dve.wait_ge(S["w_hi_ready"], p + 1)
                v.tensor_tensor(wl[:, :], wraw[:, :], wh[:, :].bitcast(f32), ALU.subtract
                                ).then_inc(S["w_lo_ready"], 1)

            def prep(kind, s, p, pb, step):
                if step == 0:
                    v.tensor_scalar(U2[:, :], head_of, uc[:, 0, bass.ds(p, 1)], None, ALU.mult
                                    ).then_inc(S["u2_ready"], 1)
                elif step in (7, 9):
                    t = (step - 7) // 2
                    dve.wait_ge(S["rs_ready"], 2 * p + t + 1)
                    v.scalar_tensor_tensor(RAW[:, t, :], RAW[:, t, :], qwk[:, 2 - t:3 - t], SQ[:, t, :],
                                           op0=ALU.mult, op1=ALU.mult).then_inc(S["qk_ready"], 1)
                elif step == 10:
                    o, free = taken(kind, s, "gate")
                    v.tensor_copy(GT[:, 0, :], o[:, 0:2 * TB]).then_inc(S["gl_ready"], 1)
                    dve.wait_ge(S["gl_ready"], p + 1)
                    dve.sem_inc(free, 1)

            def prep_values(kind, s, p, pb, step):
                if step == 1:
                    wait(dve, S["pv_done"], NC * (2 * p - 2))
                    o, free = taken(kind, s, "aug1")
                    for a in range(2):
                        v.tensor_copy(KM[pb][AUG:AUG + 32, a, CH:T], o[AUG + 32 * a:AUG + 32 * a + 32, :]
                                      ).then_inc(S["bias_rows_1"], 1)
                    dve.wait_ge(S["bias_rows_1"], 2 * p + 2)
                    dve.sem_inc(free, 1)
                elif step - 1 in VALUES:
                    c = VALUES.index(step - 1)
                    o, free = taken(kind, s, f"v{c}")
                    dve.wait_ge(S["v_hi_ready"], 2 * p + c + 1)
                    blocks = slice(4 * c, 4 * c + 4)
                    v.tensor_tensor(VL[pb][:, blocks, :, 0:D], o.rearrange("p (j a d) -> p j a d", j=4, a=2),
                                    VH[pb][:, blocks, :, 0:D].bitcast(f32), ALU.subtract
                                    ).then_inc(S["v_ready"], 1)
                    dve.wait_ge(S["v_ready"], 2 * p + c + 1)
                    dve.sem_inc(free, 1)
                    if c == 1:
                        split_weights(p + 1)

            def max_chunk(n, i):
                ib, j0, w, _ = MAXC[i]
                dve.wait_ge(S["max_scores"], NC * n + i + 1)
                o = mcol[:, ib:ib + 1] if ib < 4 else mx[:, ib - 4, j0 // CH:j0 // CH + 1]
                if i == 0:
                    wait(dve, S["mrow_ready"], n)
                last = v.tensor_reduce(o, SM[:, i % 2, 0:w], axis=AX.X, op=ALU.max).then_inc(S["max_taken"], 1)
                if i == NC - 1:
                    dve.wait_ge(S["max_taken"], NC * (n + 1))
                    v.tensor_tensor(mcol[:, 4:8], mx[:, :, 0], mx[:, :, 1], ALU.max).then_inc(S["max_ready"], 1)

            def split_probs(n, i):
                w = STC[i][3]
                hi, lo, both = PH[:, i % 4, 0:w], PL[:, i % 4, 0:w], PR[:, i % 4, 0:w]
                wait(dve, S["pv_done"], NC * n + i - 3)
                dve.wait_ge(S["probs_ready"], NC * n + i + 1)
                hi_made, count = hi_ready(n, i)
                if i not in HI_ON_ACT:
                    v.tensor_copy(hi, both).then_inc(hi_made, 1)
                dve.wait_ge(hi_made, count)
                v.tensor_tensor(lo, both, hi.bitcast(f32), ALU.subtract).then_inc(S["lo_probs"], 1)

            def normalise(n, a, p, c):
                dve.wait_ge(S["sum_inv"], 2 * n + c + 1)
                if a == 0:
                    wait(dve, S["proj_added"], 2 * p)
                half = slice(c * CH, (c + 1) * CH)
                v.tensor_tensor(Y[D * a:D * a + D, half], AV[0:D, half], RL[:, half], ALU.mult
                                ).then_inc(S["y_ready"], 1)

            def add_projection(kind, s, p, halves):
                for c in halves:
                    o, free = taken(kind, s, f"pr{c}")
                    dst = acc[:, bass.ds(batch(p) * T + c * CH, CH)]
                    v.tensor_tensor(dst, o, dst, ALU.add).then_inc(S["proj_added"], 1)
                    dve.wait_ge(S["proj_added"], 2 * p + c + 1)
                    dve.sem_inc(free, 1)

            def moe_step(kind, s, b, step):
                if step == 6:
                    bank, ready, _ = use(kind, s, "mgu")
                    up = XB[0:F, bank, 2 * CAP:4 * CAP]
                    gt = XB[0:F, bank, 0:2 * CAP]
                    dve.wait_ge(S["sg_exp"], 3 * s + 3)
                    v.tensor_tensor(SG[:, 1, :], gt, SG[:, 0, :], ALU.mult).then_inc(S["sg"], 1)
                    dve.wait_ge(S["sg"], s + 1)
                    v.tensor_tensor(SG[:, 2, :], up, SG[:, 1, :], ALU.mult).then_inc(S["h_ready"], 1)
                    dve.wait_ge(S["h_ready"], s + 1)
                    dve.sem_inc(spare_free[bank], 1)
                elif step == 8:
                    o, free = taken(kind, s, "meo")
                    wait(dve, S["scatter_done"], 32 * s)
                    for e in range(2):
                        last = v.tensor_scalar(YW[:, e, :], o[:, e * C:(e + 1) * C],
                                               G[b][:, e, bass.ds(2 * s + (C + e), 1)], None, ALU.mult)
                    last.then_inc(S["yw_ready"], 1)
                    dve.wait_ge(S["yw_ready"], s + 1)
                    dve.sem_inc(free, 1)

            count = [0]

            def rt(ins):
                count[0] += 1
                ins.then_inc(S["rt"], 1)
                dve.wait_ge(S["rt"], count[0])

            dve.wait_ge(S["x_in"], 16)
            for t in range(NT):
                v.bn_stats(stats[:, t, :], X[:, t, :]).then_inc(S["stats_ready"], 1)
            dve.wait_ge(S["stats_ready"], NT)
            for t in range(NT):
                v.bn_aggr(mv[:, t, :], stats[:, t, :]).then_inc(S["ln_var"], 1)
            dve.wait_ge(S["const_in"], 16 * 8)
            v.tensor_copy(maskb[:, 0:P], ident)
            v.tensor_copy(maskb[:, P:3 * P], masks).then_inc(S["mask_ready"], 1)
            rt(v.tensor_tensor(uc[:, 1, :], uc[:, 0, :], uc[:, 0, :], ALU.mult))
            dve.sem_inc(S["u_sq"], 1)
            dve.sem_inc(S["consts_ready"], 1)
            rt(v.tensor_scalar(qwk[:, 2:3], qwk[:, 0:1], 0.125, None, ALU.mult))
            dve.wait_ge(S["ln_rstd"], 2)
            dve.wait_ge(S["ln_var"], NT)
            for t in range(NT):
                last = v.tensor_scalar(XW[:, t, 0:C], X[:, t, :], mv[:, t, 0:1], rs[:, 1, t:t + 1],
                                       ALU.subtract, ALU.mult)
                if t % 4 == 3:
                    last.then_inc(S["xn_ready"], 1)
            dve.wait_ge(S["u_psum"], 1)
            v.tensor_scalar(uc[:, 1, :], AV[:, 0:NPAIR], float(D), 1e-12, ALU.mult, ALU.max).then_inc(S["u_ln"], 1)
            for g in range(4):
                dve.wait_ge(S["xt_psum"], g + 1)
                v.tensor_copy(xf[:, g * CH:(g + 1) * CH], ST[:, g % 2, :]).then_inc(S["xt_copied"], 1)
            dve.wait_ge(S["u_ln"], 3)
            rt(v.tensor_scalar(uc[:, 1, :], uc[:, 1, :], 0.125, None, ALU.mult))
            v.tensor_tensor(uc[:, 0, :], uc[:, 0, :], uc[:, 1, :], ALU.mult).then_inc(S["u_ready"], 1)
            dve.wait_ge(S["u_ready"], 1)
            dve.wait_ge(S["omega_exp"], 3)
            rt(v.scalar_tensor_tensor(omE[:, 2, :], omE[:, 0, :], 0.0, omE[:, 1, :], op0=ALU.max, op1=ALU.add))
            rt(v.tensor_tensor(omE[:, 0, :], omE[:, 2, :], slopes, ALU.mult))
            split_weights(0)
            for g in range(4):
                dve.wait_ge(S["xh_ready"], g + 1)
                v.tensor_tensor(xl[:, g * CH:(g + 1) * CH], xf[:, g * CH:(g + 1) * CH],
                                xh[:, g * CH:(g + 1) * CH].bitcast(f32), ALU.subtract).then_inc(S["xl_ready"], 1)
            dve.wait_ge(S["logit_psum"], 1)
            lg = SM[:, 0, :].rearrange("p (t e) -> p t e", e=E)
            rt(v.tensor_reduce(rsum[:, 0, :], lg, axis=AX.X, op=ALU.max))
            v.tensor_tensor(chosen, lg, rsum[:, 0, :].unsqueeze(2).to_broadcast([P, NT, E]), ALU.subtract
                            ).then_inc(S["rt_exp"], 1)

            def choose():
                dve.wait_ge(S["table_out"], 16)
                dve.wait_ge(S["total_out"], 32)
                dve.wait_ge(S["rt_exp"], 2)
                for t in range(NT):
                    v.max(tops[:, t, :], prob[:, t, :]).then_inc(S["logit_done"], 1)
                dve.wait_ge(S["logit_done"], NT)
                for t in range(NT):
                    v.match_replace(repl[:, t, :], tops[:, t, :], prob[:, t, :], -1.0).then_inc(S["logit_done"], 1)
                dve.wait_ge(S["logit_done"], 2 * NT)
                rt(v.tensor_scalar(chosen, repl, 0.0, None, ALU.is_lt))
                for g in range(4):
                    last = v.tensor_copy(selr[:, :, g, :], chosen)
                last.then_inc(S["selr_ready"], 1)

            def weights():
                rt(v.tensor_tensor(repl, prob, chosen, ALU.mult))
                rt(v.tensor_reduce(rsum[:, 1, :], repl, axis=AX.X, op=ALU.add))
                rt(v.reciprocal(rsum[:, 2, :], rsum[:, 1, :]))
                v.tensor_tensor(XW[:, :, C:ROW], repl, rsum[:, 2, :].unsqueeze(2).to_broadcast([P, NT, E]), ALU.mult
                                ).then_inc(S["wts_ready"], 1)

            def counts():
                v.tensor_copy(CUM[:, N:N + CAP], slot_no)
                rt(v.memset(ONES, 1.0))
                for g in range(4):
                    dve.wait_ge(S["selT_psum"], g + 1)
                    v.tensor_tensor_scan(CUM[:, g * CH:(g + 1) * CH], ONES, (ST, SM)[g // 2][:, g % 2, :],
                                         0.0 if g == 0 else CUM[:, g * CH - 1:g * CH],
                                         ALU.mult, ALU.add).then_inc(S["selT_done"], 1)
                    dve.wait_ge(S["selT_done"], g + 1)

            def find_slots(h):
                last = v.max_index(idx[:, 8 * h:8 * h + 8], own_slot_no[:, 8 * h:8 * h + 8], CUM)
                if h == 3:
                    rt(last)
                    v.transpose(idxT[:, :], idx[:, :]).then_inc(S["idx_ready"], 1)

            prep("PRO", 0, 0, 0, 0)
            choose()
            for step in range(1, NC):
                prep("PRO", 0, 0, 0, step)
                if step == 7:
                    weights()
                if step == 9:
                    counts()
            dve.wait_ge(S["bias_zero"], 1)
            gate_bias(0)
            find_slots(0)
            for step in range(VALUES[0]):
                prep_values("PRO", 0, 0, 0, step)
                if step == 1:
                    find_slots(1)
            for i in range(NC):
                max_chunk(0, i)
            find_slots(2)
            for step in VALUES:
                prep_values("PRO", 0, 0, 0, step + 1)
            find_slots(3)

            def slot(s, b, a, kind, nxt):
                n = 2 * s + a
                first = FIRST_MAX[a]
                for i in range(NC):
                    if a == 1 and i == 0 and kind != "LAST":
                        gate_bias(s + 1)
                    if i >= 1:
                        split_probs(n, i - 1)
                    elif not (kind == "FIRST" and a == 0):
                        split_probs(n - 1, NC - 1)
                    if nxt and first <= i < first + 6:
                        max_chunk(n + 1, 2 * (i - first))
                        max_chunk(n + 1, 2 * (i - first) + 1)
                    if i == SUMS[1] + 1 and not (kind == "FIRST" and a == 0):
                        normalise(n - 1, 1 - a, s - 1 if a == 0 else s, 1)
                    if a == 0 and kind != "LAST":
                        prep(kind, s, s + 1, 1 - b, i)
                    if a == 0 and i in PROJECT and kind != "FIRST":
                        add_projection(kind, s, s - 1, (PROJECT.index(i),))
                    if a == 1:
                        moe_step(kind, s, b, i)
                        if kind != "LAST":
                            prep_values(kind, s, s + 1, 1 - b, i)
                    if i == SUMS[0] + 1:
                        normalise(n, a, s, 0)

            def period(s, b, kind):
                slot(s, b, 0, kind, True)
                slot(s, b, 1, kind, kind != "LAST")

            period(0, 0, "FIRST")
            dve.wait_ge(S["acc_zero"], 1)
            with dve.Fori(0, (NPAIR - 2) // 2) as it:
                period(2 * it + 1, 1, "MID")
                period(2 * it + 2, 0, "MID")
            period(NPAIR - 1, 1, "LAST")
            split_probs(2 * NPAIR - 1, NC - 1)
            normalise(2 * NPAIR - 1, 1, NPAIR - 1, 1)
            add_projection("FIN", 0, NPAIR - 1, (0, 1))
            dve.wait_ge(S["res_in"], 16)
            for g in range(4):
                o, free = taken("FIN", 0, f"ft{g}")
                v.tensor_tensor(fin[:, 4 * g:4 * g + 4, :], o.rearrange("p (t c) -> p t c", c=C),
                                res[:, 4 * g:4 * g + 4, :], ALU.add).then_inc(S["final_ready"], 1)
                dve.wait_ge(S["final_ready"], g + 1)
                dve.sem_inc(free, 1)

        @block.gpsimd
        def _(pool):
            g_ = nc.gpsimd

            def stand(value):
                if not isinstance(value, int):
                    pool.sem_inc(S["pool_steps"], 1)
            g_.memset(ZR[:, :], 0.0).then_inc(S["zero_ready"], 1)
            g_.memset(eps[:, :], 1e-5).then_inc(S["eps_ready"], 2)
            for b in range(2):
                g_.memset(VH[b][:, :, :, D:2 * D].bitcast(f32), 1.0)
                last = g_.memset(VL[b][:, :, :, D:2 * D].bitcast(f32), 0.0)
            last.then_inc(S["v_ones"], 1)
            pool.wait_ge(S["const_in"], 16 * 8)
            g_.tensor_copy(rows[:, :], rows_f).then_inc(S["rows_ready"], 1)
            pool.wait_ge(S["rows_ready"], 1)
            g_.memset(R, 0.0).then_inc(S["bias_zero"], 1)

            def split(p):
                for t, done in ((0, S["lo_q_ready"]), (1, S["lo_k_ready"])):
                    pool.wait_ge(S["hi_ready"], 2 * p + t + 1)
                    stand(p)
                    g_.tensor_tensor(LO[:, t, :], RAW[:, t, :], HI[:, t, :].bitcast(f32), ALU.subtract
                                     ).then_inc(done, 1)

            def gather(s, b):
                if not isinstance(s, int) or s >= 2:
                    pool.wait_ge(S["yw_ready"], s - 1)
                    stand(s)
                g_.tensor_copy(idxc[b][:, :], idxT[:, bass.ds(2 * s, 2)]).then_inc(S["idxc_ready"], 1)
                pool.wait_ge(S["idxc_ready"], s + 1)
                stand(s)
                for e in range(2):
                    g_.indirect_dma_start(out=G[b][:, e, :], out_offset=None, in_=table,
                                          in_offset=bass.IndirectOffsetOnAxis(ap=idxc[b][:, e:e + 1], axis=0)
                                          ).then_inc(S["gather_in"], 16)
                pool.wait_ge(S["gather_in"], 32 * (s + 1))
                stand(s)

            def scatter(s, b):
                pool.wait_ge(S["yw_ready"], s + 1)
                stand(s)
                for e in range(2):
                    g_.indirect_dma_start(out=total,
                                          out_offset=bass.IndirectOffsetOnAxis(ap=idxc[b][:, e:e + 1], axis=0),
                                          in_=YW[:, e, :], in_offset=None, compute_op=ALU.add
                                          ).then_inc(S["scatter_done"], 16)
                    pool.wait_ge(S["scatter_done"], 32 * s + 16 * (e + 1))
                    stand(s)

            split(0)
            pool.wait_ge(S["idx_ready"], 1)
            pool.wait_ge(S["table_out"], 32)
            pool.wait_ge(S["total_out"], 32)
            gather(0, 0)
            g_.memset(acc, 0.0).then_inc(S["acc_zero"], 1)

            def period(s, b, kind):
                if kind != "LAST":
                    split(s + 1)
                scatter(s, b)
                if kind != "LAST":
                    gather(s + 1, 1 - b)

            period(0, 0, "FIRST")
            with pool.Fori(0, (NPAIR - 2) // 2) as it:
                period(2 * it + 1, 1, "MID")
                period(2 * it + 2, 0, "MID")
            period(NPAIR - 1, 1, "LAST")


_INPUTS = ("x", "w3", "wproj", "qw", "kw", "om", "u", "gwt", "gup", "dwn", "cst", "augq")


def _constants(np):
    p, q = np.arange(P)[:, None], np.arange(P)[None, :]
    k = np.zeros((P, K_ALL), np.float32)
    k[:, K_ID:K_ID + P] = p == q
    k[:, K_MR:K_MR + P] = np.where(q > p, NEG, 0.0)
    k[:, K_MT:K_MT + P] = np.where(p > q, NEG, 0.0)
    k[:, K_NP] = -np.arange(P)
    k[:, K_SLOT:K_SLOT + P] = q + 1
    k[:, K_ONES:K_ONES + P] = (p // D == q // D) / D
    k[:, K_UM:K_UM + 2] = p // D == np.arange(2)[None, :]
    k[:, K_SL:K_SL + 2 * NPAIR] = -np.tile(2.0 ** (-8.0 * (np.arange(H) + 1) / H), B)[None, :]
    k[:, K_OWN:K_OWN + CAP // 4] = 32 * (p // 32) + np.arange(1, CAP // 4 + 1)[None, :]
    a = np.zeros((MROW - AUG + 1, T), np.float32)
    i = np.arange(T)
    for t in range(TB):
        a[t] = a[TB + t] = i - P * t
    a[2 * TB:2 * TB + 2] = 1.0
    a[MROW - AUG] = 1.0
    return k, a


def kernel(L0_attn_x, L0_attn_Wq, L0_attn_Wk, L0_attn_Wv, L0_attn_Wproj, L0_attn_q_rms_w, L0_attn_k_rms_w,
           L0_attn_omega, L0_attn_u, L0_ffn_gate_weight, L0_ffn_gate_up_proj, L0_ffn_down_proj):
    import numpy as np
    import concourse.bacc as bacc
    from concourse.bass_utils import run_bass_kernel_spmd

    def pairs(w):
        return np.asarray(w).reshape(C, H // 2, 2 * D).transpose(1, 0, 2)

    cst, augq = _constants(np)
    arrays = {
        "x": np.asarray(L0_attn_x).reshape(N, C),
        "w3": np.concatenate([pairs(L0_attn_Wq), pairs(L0_attn_Wk), pairs(L0_attn_Wv)], axis=2),
        "wproj": np.asarray(L0_attn_Wproj).reshape(H // 2, 2 * D, C),
        "qw": np.tile(np.asarray(L0_attn_q_rms_w), 2)[:, None],
        "kw": np.tile(np.asarray(L0_attn_k_rms_w), 2)[:, None],
        "om": np.broadcast_to(np.tile(np.asarray(L0_attn_omega), B)[None, :], (P, 2 * NPAIR)),
        "u": np.tile(np.asarray(L0_attn_u).reshape(H // 2, 2 * D).T, (1, B)),
        "gwt": np.asarray(L0_ffn_gate_weight).T,
        "gup": np.asarray(L0_ffn_gate_up_proj).reshape(NPAIR, 2, 2 * F, C).transpose(0, 3, 1, 2).reshape(
            NPAIR, C, 4 * F),
        "dwn": np.asarray(L0_ffn_down_proj).reshape(NPAIR, 2, C, F).transpose(0, 3, 1, 2).reshape(NPAIR, F, 2 * C),
        "cst": cst,
        "augq": augq,
    }
    arrays = {k: np.ascontiguousarray(a) for k, a in arrays.items()}
    nc = bacc.Bacc("TRN2", target_bir_lowering=False, num_devices=1)
    ins = [nc.dram_tensor(f"in_{k}", arrays[k].shape, mybir.dt.from_np(arrays[k].dtype), kind="ExternalInput").ap()
           for k in _INPUTS]
    out = nc.dram_tensor("out", (N, C), mybir.dt.float32, kind="ExternalOutput").ap()
    layer(nc, *ins, out)
    r = run_bass_kernel_spmd(nc, [{f"in_{k}": a for k, a in arrays.items()}], core_ids=[0])
    return r.results[0]["out"].reshape(B, T, C)
```
